# Optimizing a Trainium2 kernel written in Bass

```python
import numpy as np
import jax
import jax.numpy as jnp

def _softmax(x, axis=-1):
    return jax.nn.softmax(x, axis=axis)
def _gelu(x):
    return jax.nn.gelu(x, approximate=True)
def _silu(x):
    return jax.nn.silu(x)
def _sigmoid(x):
    return jax.nn.sigmoid(x)
def _layernorm(x, axis=-1, eps=1e-5):
    m = jnp.mean(x, axis=axis, keepdims=True)
    v = jnp.var(x, axis=axis, keepdims=True)
    return (x - m) / jnp.sqrt(v + eps)
def _scatter_add(tgt, idx, src, axis=0):
    return tgt.at[idx].add(src)
def _segment_sum(src, seg, n):
    return jax.ops.segment_sum(src, seg, n)

kernel_name = 'mk_metaformer_d2_conv_nchw128_f904db'

def setup_inputs(seed: int = 0):
    np.random.seed(seed)
    _w = jnp.asarray
    def _rec_inputs():
        import jax
        import jax.numpy as jnp
        _gk = jax.random.key(seed)
        x = -0.0002928 + 1 * jax.random.normal(jax.random.fold_in(_gk, 1), (32, 128, 32, 32), jnp.float32)
        return x
    x = _rec_inputs()
    def _L0_conv_setup():
        import jax, jax.numpy as jnp
        import numpy as np
        BN_EPS = 1e-05

        def tanhshrink(x):
            return x - jnp.tanh(x)
        key = jax.random.key(seed)
        ks = jax.random.split(key, 10)
        B, C, H, W = (32, 128, 32, 32)
        RIN, RH, OC = (256, 512, 128)
        s = lambda k, shape, fan: jax.random.normal(k, shape, dtype=jnp.float32) * (1.0 / np.sqrt(fan))
        return {'x': jax.random.normal(ks[0], (B, C, H, W), dtype=jnp.float32), 'gamma': jnp.ones((C,), jnp.float32), 'beta': jnp.zeros((C,), jnp.float32), 'w_in': s(ks[1], (RIN, C), C), 'b_in': jnp.zeros((RIN,), jnp.float32), 'w_ih': s(ks[2], (RH, RIN), RIN), 'b_ih': jnp.zeros((RH,), jnp.float32), 'w_hh': s(ks[3], (RH, RH), RH), 'b_hh': jnp.zeros((RH,), jnp.float32), 'w_out': s(ks[4], (OC, RH), RH), 'b_out': jnp.zeros((OC,), jnp.float32)}
    _L0_conv_all = _L0_conv_setup()
    _L0_conv_in = {k: v for k, v in _L0_conv_all.items() if k in ('gamma', 'beta', 'w_in', 'b_in', 'w_ih', 'b_ih', 'w_hh', 'b_hh', 'w_out', 'b_out', )}
    del _L0_conv_all

    def _L0_ffn_setup():
        import jax, jax.numpy as jnp
        import numpy as np
        B, N, D, C, E, K = (8, 8192, 128, 128, 8, 2)
        key = jax.random.key(seed)
        k0, k1, k2 = jax.random.split(key, 3)
        x = jax.random.normal(k0, (B, N, D), dtype=jnp.float32)
        router_w = jax.random.normal(k1, (D, E), dtype=jnp.float32) * 0.05
        router_b = jnp.zeros((E,), dtype=jnp.float32)
        expert_w = jax.random.normal(k2, (E, D, C), dtype=jnp.float32) * (1.0 / np.sqrt(D))
        expert_b = jnp.zeros((E, C), dtype=jnp.float32)
        return {'x': x, 'router_w': router_w, 'router_b': router_b, 'expert_w': expert_w, 'expert_b': expert_b}
    _L0_ffn_all = _L0_ffn_setup()
    _L0_ffn_in = {k: v for k, v in _L0_ffn_all.items() if k in ('router_w', 'router_b', 'expert_w', 'expert_b', )}
    del _L0_ffn_all

    def _L1_conv_setup():
        import jax, jax.numpy as jnp
        import numpy as np
        B, C, H, W = (64, 128, 36, 100)
        KSZ = 9
        PAD = 4
        key = jax.random.key(seed)
        k1, k2 = jax.random.split(key, 2)
        x = jax.random.normal(k1, (B, C, H, W), dtype=jnp.float32)
        kernel = jax.random.normal(k2, (C, KSZ, 1, C), dtype=jnp.float32) * 0.02
        bias = jnp.zeros((C,), dtype=jnp.float32)
        return {'x': x, 'kernel': kernel, 'bias': bias}
    _L1_conv_all = _L1_conv_setup()
    _L1_conv_in = {k: v for k, v in _L1_conv_all.items() if k in ('kernel', 'bias', )}
    del _L1_conv_all

    def _L1_ffn_setup():
        import jax, jax.numpy as jnp
        import numpy as np
        BN_EPS = 1e-05
        key = jax.random.key(seed)
        k1, k2, k3 = jax.random.split(key, 3)
        B, T, I, H = (64, 2048, 128, 128)
        x = jax.random.normal(k1, (B, T, I), dtype=jnp.float32)
        W = jax.random.normal(k2, (H, I), dtype=jnp.float32) * (1.0 / np.sqrt(I))
        V = jnp.linalg.qr(jax.random.normal(k3, (H, H), dtype=jnp.float32))[0]
        gamma = jnp.ones((H,), dtype=jnp.float32)
        beta = jnp.zeros((H,), dtype=jnp.float32)
        return {'x': x, 'W': W, 'V': V, 'gamma': gamma, 'beta': beta}
    _L1_ffn_all = _L1_ffn_setup()
    _L1_ffn_in = {k: v for k, v in _L1_ffn_all.items() if k in ('W', 'V', 'gamma', 'beta', )}
    del _L1_ffn_all

    return {
        "x": x,
        "L0_conv_gamma": _L0_conv_in["gamma"],
        "L0_conv_beta": _L0_conv_in["beta"],
        "L0_conv_w_in": _L0_conv_in["w_in"],
        "L0_conv_b_in": _L0_conv_in["b_in"],
        "L0_conv_w_ih": _L0_conv_in["w_ih"],
        "L0_conv_b_ih": _L0_conv_in["b_ih"],
        "L0_conv_w_hh": _L0_conv_in["w_hh"],
        "L0_conv_b_hh": _L0_conv_in["b_hh"],
        "L0_conv_w_out": _L0_conv_in["w_out"],
        "L0_conv_b_out": _L0_conv_in["b_out"],
        "L0_ffn_router_w": _L0_ffn_in["router_w"],
        "L0_ffn_router_b": _L0_ffn_in["router_b"],
        "L0_ffn_expert_w": _L0_ffn_in["expert_w"],
        "L0_ffn_expert_b": _L0_ffn_in["expert_b"],
        "L1_conv_kernel": _L1_conv_in["kernel"],
        "L1_conv_bias": _L1_conv_in["bias"],
        "L1_ffn_W": _L1_ffn_in["W"],
        "L1_ffn_V": _L1_ffn_in["V"],
        "L1_ffn_gamma": _L1_ffn_in["gamma"],
        "L1_ffn_beta": _L1_ffn_in["beta"],
    }

def reference(x, L0_conv_gamma, L0_conv_beta, L0_conv_w_in, L0_conv_b_in, L0_conv_w_ih, L0_conv_b_ih, L0_conv_w_hh, L0_conv_b_hh, L0_conv_w_out, L0_conv_b_out, L0_ffn_router_w, L0_ffn_router_b, L0_ffn_expert_w, L0_ffn_expert_b, L1_conv_kernel, L1_conv_bias, L1_ffn_W, L1_ffn_V, L1_ffn_gamma, L1_ffn_beta):
    import jax
    import jax.numpy as jnp
    def _L0_conv_ref(x, gamma, beta, w_in, b_in, w_ih, b_ih, w_hh, b_hh, w_out, b_out):
        import jax, jax.numpy as jnp
        import numpy as np
        BN_EPS = 1e-05

        def tanhshrink(x):
            return x - jnp.tanh(x)
        B, C, H, W = x.shape
        RH = w_hh.shape[0]
        mean = jnp.mean(x, axis=(0, 2, 3), keepdims=True)
        var = jnp.var(x, axis=(0, 2, 3), keepdims=True)
        xn = (x - mean) * jax.lax.rsqrt(var + BN_EPS)
        xn = xn * gamma[None, :, None, None] + beta[None, :, None, None]
        seq = jnp.transpose(xn, (0, 2, 3, 1)).reshape(B, H * W, C)
        inp = tanhshrink(jnp.einsum('blc,ic->bli', seq, w_in) + b_in)
        xgate = jnp.einsum('bli,hi->blh', inp, w_ih) + b_ih + b_hh
        xgate_t = jnp.transpose(xgate, (1, 0, 2))

        def step(h, xg):
            h_new = jnp.tanh(xg + h @ w_hh.T)
            return (h_new, h_new)
        h0 = jnp.zeros((B, RH), x.dtype)
        _, hs = jax.lax.scan(step, h0, xgate_t)
        outputs = jnp.transpose(hs, (1, 0, 2))
        out_seq = jnp.einsum('blh,oh->blo', outputs, w_out) + b_out
        out = jnp.transpose(out_seq.reshape(B, H, W, -1), (0, 3, 1, 2))
        return out

    def _L0_ffn_ref(x, router_w, router_b, expert_w, expert_b):
        import jax, jax.numpy as jnp
        import numpy as np
        B, N, D, C, E, K = (8, 8192, 128, 128, 8, 2)
        router_probs = jax.nn.softmax(x @ router_w + router_b, axis=-1)
        top_p, top_i = jax.lax.top_k(router_probs, K)
        top_p = top_p / jnp.sum(top_p, axis=-1, keepdims=True)
        expert_out = jnp.einsum('bnd,edc->bnec', x, expert_w) + expert_b
        gathered = jnp.take_along_axis(expert_out, top_i[..., None], axis=2)
        return jnp.einsum('bnk,bnkc->bnc', top_p, gathered)

    def _L1_conv_ref(x, kernel, bias):
        import jax, jax.numpy as jnp
        import numpy as np
        B, C, H, W = (64, 128, 36, 100)
        KSZ = 9
        PAD = 4
        w = jnp.transpose(kernel[:, :, 0, :], (2, 0, 1))

        def conv_row(row):
            return jax.lax.conv_general_dilated(row, w, window_strides=(1,), padding=[(PAD, PAD)], dimension_numbers=('NCH', 'OIH', 'NCH'))

        def step(carry, x_row):
            inp = x_row + carry
            out = jax.nn.relu(conv_row(inp) + bias[None, :, None])
            return (out, out)
        x_rows = jnp.transpose(x, (2, 0, 1, 3))
        _, outs = jax.lax.scan(step, jnp.zeros_like(x_rows[0]), x_rows)
        return jnp.transpose(outs, (1, 2, 0, 3))

    def _L1_ffn_ref(x, W, V, gamma, beta):
        import jax, jax.numpy as jnp
        import numpy as np
        BN_EPS = 1e-05
        B, T, H = (x.shape[0], x.shape[1], W.shape[0])
        Wx = jnp.einsum('bti,hi->bth', x, W)
        flat = Wx.reshape(B * T, H)
        mean = jnp.mean(flat, axis=0)
        var = jnp.var(flat, axis=0)
        Wx = ((flat - mean) * jax.lax.rsqrt(var + BN_EPS) * gamma + beta).reshape(B, T, H)
        Vt = V.T

        def step(yt, wx_t):
            yt = jax.nn.sigmoid(wx_t + yt @ Vt)
            return (yt, yt)
        y0 = jnp.zeros((B, H), dtype=Wx.dtype)
        _, ys = jax.lax.scan(step, y0, jnp.swapaxes(Wx, 0, 1))
        return jnp.swapaxes(ys, 0, 1)

    def _gn(v, G=32, eps=1e-5):
        B_, C_, H_, W_ = v.shape
        g = v.reshape(B_, G, C_ // G, H_, W_)
        m = jnp.mean(g, axis=(2, 3, 4), keepdims=True)
        s = jnp.var(g, axis=(2, 3, 4), keepdims=True)
        return ((g - m) / jnp.sqrt(s + eps)).reshape(v.shape)

    def _ln_c(v, eps=1e-6):
        m = jnp.mean(v, axis=1, keepdims=True)
        s = jnp.var(v, axis=1, keepdims=True)
        return (v - m) / jnp.sqrt(s + eps)

    def _ln_t(v, eps=1e-5):
        m = jnp.mean(v, axis=-1, keepdims=True)
        s = jnp.var(v, axis=-1, keepdims=True)
        return (v - m) / jnp.sqrt(s + eps)

    def _to_tokens(v):
        B_, C_, H_, W_ = v.shape
        return v.reshape(B_, C_, H_ * W_).transpose(0, 2, 1)
    def _from_tokens(t, like):
        B_, C_, H_, W_ = like.shape
        return t.transpose(0, 2, 1).reshape(B_, C_, H_, W_)

    x = x + _L0_conv_ref(_ln_c(x), L0_conv_gamma, L0_conv_beta, L0_conv_w_in, L0_conv_b_in, L0_conv_w_ih, L0_conv_b_ih, L0_conv_w_hh, L0_conv_b_hh, L0_conv_w_out, L0_conv_b_out)
    t = _to_tokens(x)
    t = t + _L0_ffn_ref(_ln_t(t), L0_ffn_router_w, L0_ffn_router_b, L0_ffn_expert_w, L0_ffn_expert_b)
    x = _from_tokens(t, x)
    x = x + _L1_conv_ref(_ln_c(x), L1_conv_kernel, L1_conv_bias)
    t = _to_tokens(x)
    t = t + _L1_ffn_ref(_ln_t(t), L1_ffn_W, L1_ffn_V, L1_ffn_gamma, L1_ffn_beta)
    x = _from_tokens(t, x)
    return x


_drawn_inputs = setup_inputs


def setup_inputs(seed=0):
    import zlib

    import numpy as np

    out = dict(_drawn_inputs(seed))
    spreads = {'L0_conv_gamma': (1.0, 0.2),
     'L0_conv_beta': (0.0, 0.1),
     'L0_conv_b_in': (0.0, 0.1),
     'L0_conv_b_ih': (0.0, 0.1),
     'L0_conv_b_hh': (0.0, 0.1),
     'L0_conv_b_out': (0.0, 0.1),
     'L0_ffn_router_b': (0.0, 0.1),
     'L0_ffn_expert_b': (0.0, 0.1),
     'L1_conv_bias': (0.0, 0.1),
     'L1_ffn_gamma': (1.0, 0.6),
     'L1_ffn_beta': (0.0, 0.637)}
    factors = {}
    for name, (base, spread) in spreads.items():
        noise = np.random.default_rng([zlib.crc32(name.encode()), seed]).standard_normal(out[name].shape)
        drawn = base * np.exp(spread * noise) if base else spread * noise
        out[name] = jnp.asarray(drawn.astype(out[name].dtype))
    for name, factor in factors.items():
        out[name] = (out[name] * factor).astype(out[name].dtype)
    return out
```

```python
import concourse.bass as bass
from concourse import mybir
from contextlib import ExitStack

F32 = mybir.dt.float32
BF16 = mybir.dt.bfloat16
U32 = mybir.dt.uint32
ALU = mybir.AluOpType
ACT = mybir.ActivationFunctionType

B, C, HH, WW = 32, 128, 32, 32
L = HH * WW
STEPS = 4
TOK = STEPS * B
GROUPS = L // STEPS
PER_ROW = WW // STEPS
IMGS = B // PER_ROW
RIN, RH = 256, 512
KI, KH = RIN // 128, RH // 128
NE = 8
TAPS, PAD = 9, 4
EPS_C, EPS_T, EPS_BN = 1e-6, 1e-5, 1e-5

LAG = dict(z=0, rnn=1, moe=2, put=3, conv=PER_ROW + 3, ln=PER_ROW + 4, wx=PER_ROW + 5)


def stages_in(slot):
    return frozenset(s for s, lag in LAG.items() if 0 <= slot - lag < GROUPS)


def segments():
    pairs = (GROUPS + max(LAG.values()) + 1) // 2
    kind = [(stages_in(2 * p), stages_in(2 * p + 1), stages_in(2 * p + 2)) for p in range(pairs)]
    out = []
    for p in range(pairs):
        if out and kind[p] == kind[out[-1][0]]:
            out[-1][1] += 1
        else:
            out.append([p, 1])
    return [tuple(x) for x in out]


def metaformer(nc, x, w_inT, b_in, w_ihT, b_ih, w_hhT, b_hh, w_outT, b_out, gamma0, beta0,
               router_w, router_b, expert_w, expert_b, conv_w, conv_b, ffn_w, ffn_vT, gamma1, beta1,
               lt_rows, out):
    ctx = ExitStack()
    with ctx:
        def sb(name, shape, dt=F32):
            return ctx.enter_context(nc.sbuf_tensor(name, shape, dt))

        def sem(name):
            return ctx.enter_context(nc.semaphore(name))

        X = sb("X", [128, B, L])
        XR = sb("XR", [128, 2, L])
        LROW = sb("LROW", [128, 2, WW, B])
        CI = sb("CI", [128, 2, B, WW])
        Y = sb("Y", [128, B, WW])
        WHH = sb("WHH", [128, KH, RH])
        WIH = sb("WIH", [128, KI, RH])
        WIN = sb("WIN", [128, RIN])
        WINS = sb("WINS", [128, RIN])
        WOUT = sb("WOUT", [128, KH, C])
        EW = sb("EW", [128, NE * C])
        RW = sb("RW", [128, NE])
        RWC = sb("RWC", [128, NE])
        CW = sb("CW", [128, TAPS * C])
        FW = sb("FW", [128, C])
        FWT = sb("FWT", [128, C])
        VT = sb("VT", [128, C])
        EB = sb("EB", [NE, C])
        RB = sb("RB", [128, NE])
        BIN = sb("BIN", [128, KI])
        ZB = sb("ZB", [128, KI])
        BOUT = sb("BOUT", [128, 1])
        CB = sb("CB", [128, 1])
        G0, B0, G1, B1 = (sb(n, [128, 1]) for n in ("G0", "B0", "G1", "B1"))
        BX = sb("BX", [3, RH], BF16)
        ONE3 = sb("ONE3", [3, TOK], BF16)
        IDN = sb("IDN", [128, 128])
        MEANW = sb("MEANW", [128, 128])
        CEN = sb("CEN", [128, 128])
        IOTA = sb("IOTA", [128, NE])
        EPS = sb("EPS", [128, 1])
        NHALF = sb("NHALF", [128, 1])
        WXS = sb("WXS", [128, GROUPS, 6])
        MV0 = sb("MV0", [128, 2])
        MV4 = sb("MV4", [128, 2])
        R0 = sb("R0", [128, 1])
        R4 = sb("R4", [128, 1])
        SC0, SH0, SC1, SH1, TMP0, TMP1 = (sb(n, [128, 1]) for n in ("SC0", "SH0", "SC1", "SH1", "TMP0", "TMP1"))
        XIN = sb("XIN", [128, 2, TOK])
        TH = sb("TH", [128, KI, TOK])
        INP = sb("INP", [128, KI, TOK])
        H = sb("H", [128, 2, KH, STEPS, B])
        TC = sb("TC", [128, TOK])
        ACC = sb("ACC", [128, C])
        XLT = sb("XLT", [128, C])
        LTOK = sb("LTOK", [128, C])
        T3C = sb("T3C", [128, TOK])
        LC = sb("LC", [128, TOK])
        CC = sb("CC", [128, IMGS, WW + 2 * PAD])
        GP = sb("GP", [128, 128])
        GR = sb("GR", [128, NE])
        GA = sb("GA", [128, NE])
        GB = sb("GB", [128, NE])
        GT = sb("GT", [NE, TOK])
        LG = sb("LG", [128, NE])
        MX = sb("MX", [128, 8])
        IX = sb("IX", [128, 8], U32)
        IXF = sb("IXF", [128, 8])
        EX, DN, G_1, G_2 = (sb(n, [128, 1]) for n in ("EX", "DN", "G_1", "G_2"))
        ST1, ST2, ST3 = (sb(n, [128, 6]) for n in ("ST1", "ST2", "ST3"))
        MV1, MV2, MV3 = (sb(n, [128, 2]) for n in ("MV1", "MV2", "MV3"))
        V1, V2, V3, V0, V4 = (sb(n, [128, 1]) for n in ("V1", "V2", "V3", "V0", "V4"))
        R1, R2, R3 = (sb(n, [128, 1]) for n in ("R1", "R2", "R3"))

        bank = [ctx.enter_context(nc.psum_tensor(f"bank{i}", [128, 512], F32)) for i in range(8)]
        XG = [bank[i][:, :].rearrange("p (m s b) -> p m s b", m=KH, s=STEPS) for i in range(2)]
        EPS_BANKS = [bank[2], bank[3]]
        bZ, bC, bT, bM = bank[4], bank[5], bank[6], bank[7]

        WXSF = WXS[:, :, :].rearrange("p t s -> p (t s)")
        BR = WXSF[0:1, 0:2 * RH].rearrange("p (a n) -> p a n", a=2)
        BHI = WXSF[0:1, 1024:1280].bitcast(BF16)
        BMID = WXSF[0:1, 1280:1536].bitcast(BF16)
        BLO = TH[0:1, :, :].rearrange("p k n -> p (k n)").bitcast(BF16)
        STAT0 = H[:, 0, :, :, :].rearrange("p k s b -> p (k s b)")[:, 0:64 * 6].rearrange("p (t s) -> p t s", s=6)
        FWS, FWST = T3C, LC
        SQ = CI[:, :, :, :].rearrange("p a b w -> p (a b w)").rearrange("p (u n) -> p u n", u=4)
        SD = LROW[:, :, :, :].rearrange("p a w b -> p (a w b)").rearrange("p (u n) -> p u n", u=4)
        RS = XR[:, :, :].rearrange("p a n -> p (a n)").rearrange("p (u n) -> p u n", u=4)
        EWRAW = Y[:, :, :].rearrange("p b w -> p (b w)")
        XF = X[:, :, :].rearrange("p b l -> p (b l)")
        YS = Y[:, :, :].rearrange("p b w -> p (b w)").rearrange("p (w b) -> p w b", w=WW)

        x_ld = [sem(f"x_ld{i}") for i in range(8)]
        w_ld = sem("w_ld")
        b3_ld = sem("b3_ld")
        consts = sem("consts")
        pool_own, dve_own = sem("pool_own"), sem("dve_own")
        (xc_ps, sq_ready, var_ps, sd_ready, norm_done, ewc_ps, ewc_sb, mv0_ready, r0_ready, zb_ps, sh0_ready,
         zb_ready, h_zero, ys_zero, fwt_ps, fwt_sb) = (sem(n) for n in (
             "xc_ps", "sq_ready", "var_ps", "sd_ready", "norm_done", "ewc_ps", "ewc_sb", "mv0_ready", "r0_ready",
             "zb_ps", "sh0_ready", "zb_ready", "h_zero", "ys_zero", "fwt_ps", "fwt_sb"))
        b_split, b_rows = sem("b_split"), sem("b_rows")
        (xin_ready, z_ps, th_ready, inp_ready, pre_ready, tanh_done, o_ps, tc_ready, t1_ps, rt_ps, moe_ps,
         mv1_ready, r1_ready, mx_ready, e_ready, g_ready, gt_ps, gt_sb, acc_ps, acc_sb, comb_done, mv2_ready,
         r2_ready, xlt_ready, t23_ps, xl_sb, cc_ready, conv_ps, y_ready, t3c_ready, t4_ps, mv3_ready, r3_ready,
         l_tok, t5_ps, lc_sb, wx_ps, wxs, lrow, spilled, xr_ld) = (sem(n) for n in (
             "xin_ready", "z_ps", "th_ready", "inp_ready", "pre_ready", "tanh_done", "o_ps", "tc_ready", "t1_ps",
             "rt_ps", "moe_ps", "mv1_ready", "r1_ready", "mx_ready", "e_ready", "g_ready", "gt_ps", "gt_sb",
             "acc_ps", "acc_sb", "comb_done", "mv2_ready", "r2_ready", "xlt_ready", "t23_ps", "xl_sb", "cc_ready",
             "conv_ps", "y_ready", "t3c_ready", "t4_ps", "mv3_ready", "r3_ready", "l_tok", "t5_ps", "lc_sb",
             "wx_ps", "wxs", "lrow", "spilled", "xr_ld"))
        (mv4_ready, r4_ready, fws_ready, fwst_ps, fwst_sb, lr_ld, wx2_ps, pre2, y2, added, stored) = (
            sem(n) for n in ("mv4_ready", "r4_ready", "fws_ready", "fwst_ps", "fwst_sb", "lr_ld", "wx2_ps", "pre2",
                             "y2", "added", "stored"))

        (pv1, pv2, pv3, x3_ready, comb, st1, st2, st3, lg, gate, gr_ready, rs_own, xn_own) = (sem(n) for n in (
            "pv1", "pv2", "pv3", "x3_ready", "comb", "st1", "st2", "st3", "lg", "gate", "gr_ready", "rs_own", "xn_own"))

        SEGS = segments()
        weights = [(WHH[:, :, :], w_hhT), (WIH[:, :, :], w_ihT), (WIN[:, :], w_inT), (WOUT[:, :, :], w_outT),
                   (EWRAW, expert_w), (RW[:, :], router_w), (CW[:, :], conv_w), (FW[:, :], ffn_w), (VT[:, :], ffn_vT),
                   (EB[:, :], expert_b), (BIN[:, :], b_in), (BOUT[:, :], b_out), (CB[:, :], conv_b),
                   (G0[:, :], gamma0), (B0[:, :], beta0), (G1[:, :], gamma1), (B1[:, :], beta1),
                   (BR[:, 0, :], b_ih), (BR[:, 1, :], b_hh), (RB[:, :], router_b.partition_broadcast(128))]
        W_LD = 16 * len(weights)

        sp_waits, pool_waits, dve_waits = sem("sp_waits"), sem("pool_waits"), sem("dve_waits")

        def wait_first(eng, s, value, count):
            eng.wait_ge(s, value)
            eng.sem_inc(count, 1)

        block = ctx.enter_context(nc.Block())

        def run(body):
            def over(eng):
                for p0, n in SEGS:
                    def pair(p, base):
                        for s in (0, 1):
                            body(p * 2 + s, s, stages_in(base + s), stages_in(base + s + 1))
                    if n == 1:
                        pair(p0, 2 * p0)
                    else:
                        with eng.Fori(p0, p0 + n) as p:
                            pair(p, 2 * p0)
            return over

        @block.sync
        def _(sp):
            nb = B // len(x_ld)
            for i in range(len(x_ld)):
                sp.dma_start(X[:, nb * i:nb * i + nb, :],
                             x[nb * i:nb * i + nb, :, :].rearrange("b c l -> c b l")).then_inc(x_ld[i], 16)

            def some_row(r):
                return r & (HH - 1)

            def xr_load(r):
                wait_first(sp, xr_ld, 16 * r, sp_waits)
                sp.dma_start(xr_row(r), x_row(r)).then_inc(xr_ld, 16)

            def xr_row(r):
                return XR[:, bass.ds(r & 1, 1), :].rearrange("p a (b w) -> p (a b) w", b=B)

            def x_row(r):
                return x[:, :, bass.ds(some_row(r) * WW, WW)].rearrange("b c w -> c b w")

            def spill(r):
                wait_first(sp, lrow, PER_ROW * (r + 1), sp_waits)
                wait_first(sp, spilled, 16 * (r + 2), sp_waits)
                sp.dma_start(lt_rows[bass.ds(some_row(r), 1), :, :].rearrange("r c n -> (r c) n"),
                             LROW[:, bass.ds(r & 1, 1), :, :].rearrange("p a w b -> p (a w b)")).then_inc(spilled, 16)

            wait_first(sp, norm_done, 64, sp_waits)
            for r in range(4):
                if r >= 2:
                    wait_first(sp, tc_ready, PER_ROW * (r - 1), sp_waits)
                xr_load(r)
            with sp.Fori(0, HH - 4) as r:
                spill(r)
                wait_first(sp, tc_ready, PER_ROW * (r + 3), sp_waits)
                xr_load(r + 4)
            for r in range(HH - 4, HH):
                spill(r)
                if r == HH - 4:
                    wait_first(sp, tc_ready, GROUPS, sp_waits)
            wait_first(sp, spilled, 16 * (HH + 2), sp_waits)

            def lr_load(r):
                wait_first(sp, lr_ld, 16 * r, sp_waits)
                sp.dma_start(XR[:, bass.ds(r & 1, 1), :].rearrange("p a n -> p (a n)"),
                             lt_rows[bass.ds(some_row(r), 1), :, :].rearrange("r c n -> (r c) n")).then_inc(lr_ld, 16)
            lr_load(0)
            lr_load(1)

            def four_rows(q, loads):
                for u in range(loads):
                    wait_first(sp, wx2_ps, 8 * q + 2 * u + 2, sp_waits)
                    lr_load(q * 4 + u + 2)
                wait_first(sp, added, 8 * q + 8, sp_waits)
                sp.dma_start(out[:, :, bass.ds((q & 7) * 4 * WW, 4 * WW)].rearrange("b c l -> c b l"),
                             X[:, :, bass.ds((q & 7) * 4 * WW, 4 * WW)]).then_inc(stored, 16)
            with sp.Fori(0, HH // 4 - 1) as q:
                four_rows(q, 4)
            four_rows(HH // 4 - 1, 2)
            wait_first(sp, stored, 16 * (HH // 4), sp_waits)

        @block.gpsimd
        def _(pool):
            own = [0]

            def link(ins):
                own[0] += 1
                ins.then_inc(pool_own, 1)
                pool.wait_ge(pool_own, own[0])

            nc.gpsimd.memset(MEANW[:, :], 1.0 / C).then_inc(consts, 1)
            nc.gpsimd.memset(EPS[:, :], EPS_C).then_inc(consts, 1)
            link(nc.gpsimd.memset(IDN[:, :], 0.0))
            link(nc.gpsimd.affine_select(out=IDN[:, :], in_=IDN[:, :], compare_op=ALU.not_equal, fill=1.0, base=0,
                                         pattern=[[-1, 128]], channel_multiplier=1))
            nc.gpsimd.tensor_scalar(CEN[:, :], IDN[:, :], -1.0 / C, None, ALU.add).then_inc(consts, 1)
            for e in range(NE):
                nc.gpsimd.memset(IOTA[:, e:e + 1], float(e)).then_inc(consts, 1)
            nc.gpsimd.memset(ONE3[:, :], 1.0).then_inc(consts, 1)
            nc.gpsimd.memset(CC[:, :, :], 0.0).then_inc(consts, 1)
            nc.gpsimd.memset(GP[:, :], 0.0).then_inc(consts, 1)
            nc.gpsimd.memset(H[:, 1, :, :, :], 0.0).then_inc(consts, 1)
            link(nc.gpsimd.memset(NHALF[:, :], -0.5))

            def rstd(r, v, mv, eps, ready):
                link(nc.gpsimd.tensor_scalar(v[:, :], mv[:, 1:2], eps, None, ALU.add))
                nc.gpsimd.tensor_tensor(r[:, :], v[:, :], NHALF[:, :], ALU.pow).then_inc(ready, 1)

            pool.wait_ge(ewc_sb, 3)
            nc.gpsimd.memset(Y[:, :, :], 0.0).then_inc(ys_zero, 1)
            nc.gpsimd.memset(V3[:, :], 0.0).then_inc(spilled, 16)
            nc.gpsimd.memset(V2[:, :], 0.0).then_inc(spilled, 16)
            pool.wait_ge(mv0_ready, 1)
            rstd(R0, V0, MV0, EPS_BN, r0_ready)

            def gather(i, s):
                nc.gpsimd.tensor_copy(XIN[:, s, :].rearrange("p (s b) -> p s b", s=STEPS),
                                      X[:, :, bass.ds((i & (GROUPS - 1)) * STEPS, STEPS)].rearrange("p b s -> p s b")
                                      ).then_inc(xin_ready, 1)

            pool.wait_ge(norm_done, 64)
            gather(0, 0)

            pool.wait_ge(ys_zero, 1)

            def slot(i, s, on, nxt):
                q, l, n, o = i - LAG["conv"], i - LAG["ln"], i - LAG["put"], i - LAG["moe"]
                if "conv" in on:
                    if "put" in on:
                        pool.wait_ge(xl_sb, n)
                    else:
                        pool.wait_ge(xl_sb, GROUPS)
                    pool.wait_ge(conv_ps, q)
                    pool.wait_ge(y_ready, q)
                    b0 = (q & (PER_ROW - 1)) * IMGS
                    row = (q >> 3) & (HH - 1)
                    nc.gpsimd.tensor_tensor(
                        CC[:, :, PAD:PAD + WW],
                        CI[:, :, :, :].rearrange("p a b w -> p (a b) w")[:, bass.ds((row & 1) * B + b0, IMGS), :],
                        Y[:, bass.ds(b0, IMGS), :], ALU.add).then_inc(cc_ready, 1)
                if "z" in nxt:
                    wait_first(pool, z_ps, i, pool_waits)
                    gather(i + 1, 1 - s)
                if "put" in on:
                    wait_first(pool, mv2_ready, n + 1, pool_waits)
                    nc.gpsimd.tensor_scalar(V2[:, :], MV2[:, 1:2], EPS_C, None, ALU.add).then_inc(pv2, 1)
                    pool.wait_ge(pv2, n + 1)
                    nc.gpsimd.tensor_tensor(R2[:, :], V2[:, :], NHALF[:, :], ALU.pow).then_inc(r2_ready, 1)
                if "ln" in on:
                    wait_first(pool, mv3_ready, l + 1, pool_waits)
                    nc.gpsimd.tensor_scalar(V3[:, :], MV3[:, 1:2], EPS_T, None, ALU.add).then_inc(pv3, 1)
                    pool.wait_ge(pv3, l + 1)
                    nc.gpsimd.tensor_tensor(R3[:, :], V3[:, :], NHALF[:, :], ALU.pow).then_inc(r3_ready, 1)
                if "moe" in on:
                    wait_first(pool, mv1_ready, o + 1, pool_waits)
                    nc.gpsimd.tensor_scalar(V1[:, :], MV1[:, 1:2], EPS_T, None, ALU.add).then_inc(pv1, 1)
                    pool.wait_ge(pv1, o + 1)
                    nc.gpsimd.tensor_tensor(R1[:, :], V1[:, :], NHALF[:, :], ALU.pow).then_inc(r1_ready, 1)
                if "conv" in on:
                    pool.wait_ge(y_ready, q + 1)
                    pool.wait_ge(t4_ps, q)
                    b0 = (q & (PER_ROW - 1)) * IMGS
                    row = (q >> 3) & (HH - 1)
                    here = X[:, bass.ds(b0, IMGS), bass.ds(row * WW, WW)]
                    t3 = T3C[:, :].rearrange("p (b w) -> p b w", b=IMGS)
                    nc.gpsimd.tensor_tensor(t3, here, Y[:, bass.ds(b0, IMGS), :], ALU.add).then_inc(t3c_ready, 1)
                    wait_first(pool, t3c_ready, q + 1, pool_waits)
                    nc.gpsimd.tensor_copy(here, t3).then_inc(x3_ready, 1)
                if "ln" in on:
                    pool.wait_ge(lc_sb, l + 1)
                    row = (l >> 3) & (HH - 1)
                    wait_first(pool, spilled, 16 * row + 16, pool_waits)
                    nc.gpsimd.tensor_copy(
                        LROW[:, :, :, :].rearrange("p a w b -> p (a w) b")[
                            :, bass.ds((row & 1) * WW, WW), bass.ds((l & (PER_ROW - 1)) * IMGS, IMGS)],
                        LC[:, :].rearrange("p (b w) -> p w b", b=IMGS)).then_inc(lrow, 1)

            run(slot)(pool)
            pool.wait_ge(x3_ready, GROUPS)
            nc.gpsimd.memset(YS[:, WW - 1, :], 0.0).then_inc(y2, 1)
            pool.wait_ge(mv4_ready, 1)
            rstd(R4, V4, MV4, EPS_BN, r4_ready)

        @block.scalar
        def _(act):
            for dst, src in weights:
                act.dma_start(dst, src).then_inc(w_ld, 16)
            act.wait_ge(consts, 3)

            for seg in range(8):
                with act.Fori(seg * 2, seg * 2 + 2) as k:
                    def square(u):
                        act.wait_ge(xc_ps, k * 4 + u + 1)
                        nc.scalar.activation(SQ[:, u, :], bank[u][:, :], ACT.Square).then_inc(sq_ready, 1)

                    def sd(u):
                        act.wait_ge(var_ps, k * 4 + u + 1)
                        nc.scalar.activation(SD[:, u, :], bank[4 + u][:, :], ACT.Sqrt, bias=EPS[:, 0:1]
                                             ).then_inc(sd_ready, 1)
                    square(0)
                    square(1)
                    sd(0)
                    square(2)
                    sd(1)
                    square(3)
                    sd(2)
                    sd(3)
            act.wait_ge(b_split, 1)
            act.dma_start(BX[0:1, :], BHI[:, :]).then_inc(b_rows, 16)
            act.dma_start(BX[1:2, :], BMID[:, :]).then_inc(b_rows, 16)
            act.dma_start(BX[2:3, :], BLO[:, :]).then_inc(b_rows, 16)

            def slot(i, s, on, nxt):
                g, o, n, q, l = i - 1, i - LAG["moe"], i - LAG["put"], i - LAG["conv"], i - LAG["ln"]

                def step(t):
                    if "rnn" in on:
                        act.wait_ge(pre_ready, STEPS * g + t + 1)
                        nc.scalar.activation(H[:, 1 - s, :, t, :], XG[1 - s][:, :, t, :], ACT.Tanh
                                             ).then_inc(tanh_done, 1)
                step(0)
                if "put" in on:
                    act.wait_ge(acc_ps, n + 1)
                    act.wait_ge(t23_ps, n)
                    nc.scalar.copy(ACC[:, :], bT[:, 0:C]).then_inc(acc_sb, 1)
                if "z" in on:
                    act.wait_ge(z_ps, i + 1)
                    act.wait_ge(inp_ready, i)
                    for k in range(KI):
                        last = nc.scalar.activation(TH[:, k, :], bZ[:, k * TOK:(k + 1) * TOK], ACT.Tanh,
                                                    bias=ZB[:, k:k + 1])
                    last.then_inc(th_ready, 1)
                step(1)
                step(2)
                if "conv" in on:
                    act.wait_ge(conv_ps, q + 1)
                    nc.scalar.activation(Y[:, bass.ds((q & (PER_ROW - 1)) * IMGS, IMGS), :],
                                         bC[:, 0:TOK].rearrange("p (b w) -> p b w", b=IMGS), ACT.Relu,
                                         bias=CB[:, 0:1]).then_inc(y_ready, 1)
                if "moe" in on:
                    act.wait_ge(mx_ready, o + 1)
                    nc.scalar.activation(EX[:, :], MX[:, 0:1], ACT.Exp, scale=-1.0, bias=MX[:, 1:2]).then_inc(e_ready, 1)
                step(3)
                if "put" in on:
                    act.wait_ge(t23_ps, n + 1)
                    nc.scalar.copy(X[:, :, bass.ds((n & (GROUPS - 1)) * STEPS, STEPS)].rearrange("p b s -> p s b"),
                                   bC[:, 0:TOK].rearrange("p (s b) -> p s b", s=STEPS))
                    nc.scalar.copy(
                        CI[:, :, :, :].rearrange("p a b w -> p (a b) w")[
                            :, bass.ds(((n >> 3) & 1) * B, B), bass.ds((n & (PER_ROW - 1)) * STEPS, STEPS)
                        ].rearrange("p b s -> p s b"),
                        bC[:, TOK:2 * TOK].rearrange("p (s b) -> p s b", s=STEPS)).then_inc(xl_sb, 1)
                if "moe" in on:
                    act.wait_ge(gt_ps, o + 1)
                    nc.scalar.copy(GT[:, :], bM[0:NE, 256:256 + TOK]).then_inc(gt_sb, 1)
                if "ln" in on:
                    act.wait_ge(t5_ps, l + 1)
                    if "wx" in on:
                        act.wait_ge(wx_ps, l)
                        act.wait_ge(lrow, l)
                    nc.scalar.copy(LC[:, :], bZ[:, 384:384 + TOK]).then_inc(lc_sb, 1)

            run(slot)(act)

            act.wait_ge(fwst_sb, 1)

            def row(r, first=False):
                for w in range(WW):
                    act.wait_ge(pre2, WW * r + w + 1)
                    if w % 16 == 15 and not (first and w == 15):
                        act.wait_ge(added, 2 * r + w // 16)
                    nc.scalar.activation(YS[:, w, :], bank[w // 16][:, (w % 16) * B:(w % 16 + 1) * B], ACT.Sigmoid,
                                         bias=SH1[:, 0:1]).then_inc(y2, 1)

            row(0, first=True)
            with act.Fori(1, HH) as r:
                row(r)

        @block.vector
        def _(dve):
            own = [0]

            def link(ins):
                own[0] += 1
                ins.then_inc(dve_own, 1)
                dve.wait_ge(dve_own, own[0])

            dve.wait_ge(w_ld, W_LD)
            link(nc.vector.tensor_tensor(BR[:, 0, :], BR[:, 0, :], BR[:, 1, :], ALU.add))
            link(nc.vector.tensor_copy(BHI[:, :], BR[:, 0, :]))
            link(nc.vector.tensor_tensor(BR[:, 1, :], BR[:, 0, :], BHI[:, :], ALU.subtract))
            link(nc.vector.tensor_copy(BMID[:, :], BR[:, 1, :]))
            link(nc.vector.tensor_tensor(BR[:, 0, :], BR[:, 1, :], BMID[:, :], ALU.subtract))
            nc.vector.tensor_copy(BLO[:, :], BR[:, 0, :]).then_inc(b_split, 1)
            dve.wait_ge(ewc_ps, 1)
            nc.vector.tensor_copy(EW[:, 0:512], bank[0][:, :]).then_inc(ewc_sb, 1)
            dve.wait_ge(ewc_ps, 2)
            nc.vector.tensor_copy(EW[:, 512:1024], bank[1][:, :]).then_inc(ewc_sb, 1)
            dve.wait_ge(ewc_ps, 3)
            nc.vector.tensor_copy(RWC[:, :], bank[2][:, 0:NE]).then_inc(ewc_sb, 1)
            dve.wait_ge(ewc_ps, 4)
            nc.vector.tensor_copy(FWT[:, :], bank[3][:, 0:C]).then_inc(ewc_sb, 1)

            for seg in range(8):
                with dve.Fori(seg * 2, seg * 2 + 2) as k:
                    for u in range(4):
                        t = k * 4 + u
                        at = t & 63
                        chunk = XF[:, bass.ds(at * 512, 512)]
                        dve.wait_ge(sd_ready, t + 1)
                        nc.vector.reciprocal(RS[:, u, :], SD[:, u, :]).then_inc(rs_own, 1)
                        dve.wait_ge(rs_own, t + 1)
                        nc.vector.tensor_tensor(chunk, bank[u][:, :], RS[:, u, :], ALU.mult).then_inc(xn_own, 1)
                        dve.wait_ge(xn_own, t + 1)
                        nc.vector.bn_stats(STAT0[:, bass.ds(at, 1), :].rearrange("p t s -> p (t s)"), chunk
                                           ).then_inc(norm_done, 1)
            dve.wait_ge(norm_done, 64)
            nc.vector.bn_aggr(MV0[:, :], STAT0[:, :, :].rearrange("p t s -> p (t s)")).then_inc(mv0_ready, 1)
            dve.wait_ge(r0_ready, 1)
            link(nc.vector.tensor_tensor(SC0[:, :], G0[:, :], R0[:, :], ALU.mult))
            nc.vector.tensor_scalar(WINS[:, :], WIN[:, :], SC0[:, 0:1], None, ALU.mult)
            link(nc.vector.tensor_tensor(TMP0[:, :], MV0[:, 0:1], SC0[:, :], ALU.mult))
            nc.vector.tensor_tensor(SH0[:, :], B0[:, :], TMP0[:, :], ALU.subtract).then_inc(sh0_ready, 1)
            dve.wait_ge(zb_ps, 1)
            nc.vector.tensor_tensor(ZB[:, :], bank[7][:, 0:KI], BIN[:, :], ALU.add).then_inc(zb_ready, 1)
            dve.wait_ge(consts, 15)

            def slot(i, s, on, nxt):
                o, n, l, w = i - LAG["moe"], i - LAG["put"], i - LAG["ln"], i - LAG["wx"]
                if "moe" in on:
                    dve.wait_ge(o_ps, o + 1)
                    dve.wait_ge(xr_ld, 16 * ((o >> 3) + 1))
                    dve.wait_ge(moe_ps, o)
                    src = XR[:, :, :].rearrange("p a (b w) -> p (a b) w", b=B)[
                        :, bass.ds(((o >> 3) & 1) * B, B), bass.ds((o & (PER_ROW - 1)) * STEPS, STEPS)]
                    nc.vector.scalar_tensor_tensor(
                        TC[:, :].rearrange("p (s b) -> p s b", s=STEPS), bM[:, 0:TOK].rearrange("p (s b) -> p s b", s=STEPS),
                        BOUT[:, 0:1], src.rearrange("p b s -> p s b"), ALU.add, ALU.add).then_inc(tc_ready, 1)
                if "z" in on:
                    dve.wait_ge(th_ready, i + 1)
                    for k in range(KI):
                        last = nc.vector.scalar_tensor_tensor(
                            INP[:, k, :], bZ[:, k * TOK:(k + 1) * TOK], ZB[:, k:k + 1], TH[:, k, :],
                            ALU.add, ALU.subtract)
                    last.then_inc(inp_ready, 1)
                if "put" in on:
                    dve.wait_ge(acc_sb, n + 1)
                    dve.wait_ge(moe_ps, n + 1)
                    for e in range(NE):
                        src = EPS_BANKS[e // 4][:, (e % 4) * C:(e % 4 + 1) * C]
                        ins = nc.vector.scalar_tensor_tensor(ACC[:, :], src, GR[:, e:e + 1], ACC[:, :], ALU.mult, ALU.add)
                        if e < NE - 1:
                            ins.then_inc(comb, 1)
                            dve.wait_ge(comb, (NE - 1) * n + e + 1)
                    ins.then_inc(comb_done, 1)
                    dve.wait_ge(comb_done, n + 1)
                    nc.vector.bn_stats(ST2[:, :], ACC[:, :]).then_inc(st2, 1)
                    wait_first(dve, st2, n + 1, dve_waits)
                    nc.vector.bn_aggr(MV2[:, :], ST2[:, :]).then_inc(mv2_ready, 1)
                if "ln" in on:
                    dve.wait_ge(t4_ps, l + 1)
                    nc.vector.bn_stats(ST3[:, :], bT[:, 256:256 + C]).then_inc(st3, 1)
                    wait_first(dve, st3, l + 1, dve_waits)
                    nc.vector.bn_aggr(MV3[:, :], ST3[:, :]).then_inc(mv3_ready, 1)
                if "put" in on:
                    dve.wait_ge(r2_ready, n + 1)
                    nc.vector.tensor_scalar(XLT[:, :], ACC[:, :], MV2[:, 0:1], R2[:, 0:1], ALU.subtract, ALU.mult
                                            ).then_inc(xlt_ready, 1)
                if "ln" in on:
                    dve.wait_ge(r3_ready, l + 1)
                    nc.vector.tensor_scalar(LTOK[:, :], bT[:, 256:256 + C], MV3[:, 0:1], R3[:, 0:1],
                                            ALU.subtract, ALU.mult).then_inc(l_tok, 1)
                if "moe" in on:
                    dve.wait_ge(t1_ps, o + 1)
                    nc.vector.bn_stats(ST1[:, :], bT[:, 0:C]).then_inc(st1, 1)
                    wait_first(dve, st1, o + 1, dve_waits)
                    nc.vector.bn_aggr(MV1[:, :], ST1[:, :]).then_inc(mv1_ready, 1)
                    dve.wait_ge(rt_ps, o + 1)
                    dve.wait_ge(r1_ready, o + 1)
                    nc.vector.scalar_tensor_tensor(LG[:, :], bM[:, 128:128 + NE], R1[:, 0:1], RB[:, :],
                                                   ALU.mult, ALU.add).then_inc(lg, 1)
                    wait_first(dve, lg, o + 1, dve_waits)
                    nc.vector.max(MX[:, :], LG[:, :]).then_inc(mx_ready, 1)
                    wait_first(dve, mx_ready, o + 1, dve_waits)
                    nc.vector.max_index(IX[:, :], MX[:, :], LG[:, :]).then_inc(gate, 1)
                    dve.wait_ge(gate, 5 * o + 1)
                    dve.wait_ge(e_ready, o + 1)
                    nc.vector.tensor_copy(IXF[:, :], IX[:, :])
                    nc.vector.tensor_scalar(DN[:, :], EX[:, :], 1.0, None, ALU.add).then_inc(gate, 1)
                    dve.wait_ge(gate, 5 * o + 2)
                    nc.vector.reciprocal(G_1[:, :], DN[:, :]).then_inc(gate, 1)
                    dve.wait_ge(gate, 5 * o + 3)
                    nc.vector.tensor_tensor(G_2[:, :], EX[:, :], G_1[:, :], ALU.mult)
                    nc.vector.tensor_scalar(GA[:, :], IOTA[:, :], IXF[:, 0:1], G_1[:, 0:1], ALU.is_equal, ALU.mult
                                            ).then_inc(gate, 1)
                    dve.wait_ge(gate, 5 * o + 4)
                    nc.vector.tensor_scalar(GB[:, :], IOTA[:, :], IXF[:, 1:2], G_2[:, 0:1], ALU.is_equal, ALU.mult
                                            ).then_inc(gate, 1)
                    dve.wait_ge(gate, 5 * o + 5)
                    nc.vector.tensor_tensor(GP[:, 0:NE], GA[:, :], GB[:, :], ALU.add).then_inc(g_ready, 1)
                    dve.wait_ge(g_ready, o + 1)
                    nc.vector.tensor_scalar(GR[:, :], GP[:, 0:NE], R1[:, 0:1], None, ALU.mult).then_inc(gr_ready, 1)
                    dve.wait_ge(gr_ready, o + 1)
                if "wx" in on:
                    dve.wait_ge(wx_ps, w + 1)
                    nc.vector.bn_stats(WXS[:, bass.ds(w & (GROUPS - 1), 1), :].rearrange("p t s -> p (t s)"), bZ[:, 256:256 + TOK]
                                       ).then_inc(wxs, 1)

            run(slot)(dve)
            dve.wait_ge(wxs, GROUPS)
            nc.vector.bn_aggr(MV4[:, :], WXS[:, :, :].rearrange("p t s -> p (t s)")).then_inc(mv4_ready, 1)
            dve.wait_ge(r4_ready, 1)
            link(nc.vector.tensor_tensor(SC1[:, :], G1[:, :], R4[:, :], ALU.mult))
            nc.vector.tensor_scalar(FWS[:, :], FW[:, :], SC1[:, 0:1], None, ALU.mult).then_inc(fws_ready, 1)
            link(nc.vector.tensor_tensor(TMP1[:, :], MV4[:, 0:1], SC1[:, :], ALU.mult))
            link(nc.vector.tensor_tensor(SH1[:, :], B1[:, :], TMP1[:, :], ALU.subtract))
            dve.wait_ge(fwst_ps, 1)
            nc.vector.tensor_copy(FWST[:, :], bank[7][:, 0:C]).then_inc(fwst_sb, 1)

            with dve.Fori(0, HH) as r:
                for h in range(2):
                    dve.wait_ge(y2, WW * r + 16 * (h + 1) + 1)
                    here = X[:, :, bass.ds((r & (HH - 1)) * WW + 16 * h, 16)]
                    nc.vector.tensor_tensor(here, here, YS[:, 16 * h:16 * h + 16, :].rearrange("p w b -> p b w"),
                                            ALU.add).then_inc(added, 1)

        @block.tensor
        def _(pe):
            mm = nc.tensor.matmul
            pe.wait_ge(w_ld, W_LD)
            pe.wait_ge(consts, 3)
            for h in range(2):
                mm(bank[h][:, :], CEN[:, :], EWRAW[:, 512 * h:512 * h + 512], start=True, stop=True).then_inc(ewc_ps, 1)
            mm(bank[2][:, 0:NE], CEN[:, :], RW[:, :], start=True, stop=True).then_inc(ewc_ps, 1)
            nc.tensor.transpose(bank[3][:, 0:C], FW[:, :], IDN[:, :]).then_inc(ewc_ps, 1)
            pe.wait_ge(ewc_sb, 4)

            def four(k, first=False):
                    def centre(u):
                        if not first:
                            pe.wait_ge(norm_done, (k - 1) * 4 + u + 1)
                        mm(bank[u][:, :], CEN[:, :], XF[:, bass.ds(((k * 4 + u) & 63) * 512, 512)],
                           start=True, stop=True).then_inc(xc_ps, 1)

                    def var(u):
                        pe.wait_ge(sq_ready, k * 4 + u + 1)
                        mm(bank[4 + u][:, :], MEANW[:, :], SQ[:, u, :], start=True, stop=True).then_inc(var_ps, 1)
                    centre(0)
                    centre(1)
                    var(0)
                    centre(2)
                    var(1)
                    centre(3)
                    var(2)
                    var(3)

            pe.wait_ge(x_ld[0], 16)
            four(0, first=True)
            four(1)
            for seg in range(1, 8):
                pe.wait_ge(x_ld[seg], 16)
                with pe.Fori(seg * 2, seg * 2 + 2) as k:
                    four(k)
            pe.wait_ge(sh0_ready, 1)
            for k in range(KI):
                last = mm(bank[7][:, k:k + 1], WIN[:, k * 128:(k + 1) * 128], SH0[:, 0:1], start=True, stop=True)
            last.then_inc(zb_ps, 1)
            pe.wait_ge(zb_ready, 1)
            pe.wait_ge(b_rows, 48)
            pe.wait_ge(consts, 15)

            def slot(i, s, on, nxt):
                g, o, n = i - 1, i - LAG["moe"], i - LAG["put"]
                q, l, w = i - LAG["conv"], i - LAG["ln"], i - LAG["wx"]

                def step(t):
                    if "rnn" not in on:
                        return
                    pe.wait_ge(tanh_done, STEPS * g + t)
                    ph, pt = (s, STEPS - 1) if t == 0 else (1 - s, t - 1)
                    for m in range(KH):
                        for k in range(KH):
                            last = mm(XG[1 - s][:, m, t, :], WHH[:, k, m * 128:(m + 1) * 128], H[:, ph, k, pt, :],
                                      start=False, stop=True, skip_group_check=True)
                    last.then_inc(pre_ready, 1)

                step(0)
                if "put" in on:
                    pe.wait_ge(gt_sb, n + 1)
                    mm(bT[:, 0:C], GT[:, :], EB[:, :], start=False, stop=True, skip_group_check=True).then_inc(acc_ps, 1)
                if "moe" in on:
                    pe.wait_ge(tanh_done, STEPS * (o + 1))
                    for k in range(KH):
                        last = mm(bM[:, 0:TOK], WOUT[:, k, :], H[:, s, k, :, :].rearrange("p s b -> p (s b)"),
                                  start=(k == 0), stop=(k == KH - 1))
                    last.then_inc(o_ps, 1)
                if "z" in on:
                    pe.wait_ge(xin_ready, i + 1)
                    if "wx" in on:
                        pe.wait_ge(lc_sb, w + 1)
                    for k in range(KI):
                        last = mm(bZ[:, k * TOK:(k + 1) * TOK], WINS[:, k * 128:(k + 1) * 128], XIN[:, s, :],
                                  start=True, stop=True)
                    last.then_inc(z_ps, 1)
                step(1)
                if "ln" in on:
                    if "put" in on:
                        pe.wait_ge(acc_sb, n + 1)
                    pe.wait_ge(t3c_ready, l + 1)
                    nc.tensor.transpose(bT[:, 256:256 + C], T3C[:, :], IDN[:, :]).then_inc(t4_ps, 1)
                if "conv" in on:
                    pe.wait_ge(cc_ready, q + 1)
                    if "put" in on:
                        pe.wait_ge(xl_sb, n)
                    else:
                        pe.wait_ge(xl_sb, GROUPS)

                def taps(a, b):
                    for k in range(a, b):
                        last = mm(bC[:, 0:TOK].rearrange("p (b w) -> p b w", b=IMGS), CW[:, k * C:(k + 1) * C],
                                  CC[:, :, k:k + WW], start=(k == 0), stop=(k == TAPS - 1))
                    return last
                if "conv" in on:
                    taps(0, TAPS - 1)
                step(2)
                if "conv" in on:
                    taps(TAPS - 1, TAPS).then_inc(conv_ps, 1)
                if "moe" in on:
                    pe.wait_ge(tc_ready, o + 1)
                    if "ln" in on:
                        pe.wait_ge(l_tok, l + 1)
                    nc.tensor.transpose(bT[:, 0:C], TC[:, :], IDN[:, :]).then_inc(t1_ps, 1)
                    mm(bM[:, 128:128 + NE], TC[:, :], RWC[:, :], start=True, stop=True).then_inc(rt_ps, 1)
                    if "put" in on:
                        pe.wait_ge(comb_done, n + 1)
                    for h in range(2):
                        last = mm(EPS_BANKS[h][:, :], TC[:, :], EW[:, 512 * h:512 * h + 512], start=True, stop=True)
                    last.then_inc(moe_ps, 1)
                if "wx" in on:
                    if "z" in on:
                        pe.wait_ge(inp_ready, i + 1)
                    pe.wait_ge(lc_sb, w + 1)
                    mm(bZ[:, 256:256 + TOK], FWT[:, :], LC[:, :], start=True, stop=True).then_inc(wx_ps, 1)
                step(3)
                if "z" in on:
                    pe.wait_ge(inp_ready, i + 1)
                    for m in range(KH):
                        out_m = XG[s][:, m, :, :].rearrange("p s b -> p (s b)")
                        mm(out_m, BX[:, m * 128:(m + 1) * 128], ONE3[:, :], start=(m == 0), stop=True,
                           skip_group_check=True)
                        for k in range(KI):
                            mm(out_m, WIH[:, k, m * 128:(m + 1) * 128], INP[:, k, :], start=False, stop=True,
                               skip_group_check=True)
                if "put" in on:
                    pe.wait_ge(xlt_ready, n + 1)
                    if "conv" in on:
                        pe.wait_ge(y_ready, q + 1)
                    nc.tensor.transpose(bC[:, 0:C], ACC[:, :], IDN[:, :])
                    nc.tensor.transpose(bC[:, C:2 * C], XLT[:, :], IDN[:, :]).then_inc(t23_ps, 1)
                if "moe" in on:
                    pe.wait_ge(g_ready, o + 1)
                    nc.tensor.transpose(bM[:, 256:256 + TOK], GP[:, :], IDN[:, :]).then_inc(gt_ps, 1)
                if "ln" in on:
                    pe.wait_ge(l_tok, l + 1)
                    if "wx" in on:
                        pe.wait_ge(wxs, w + 1)
                    if "z" in on:
                        pe.wait_ge(inp_ready, i + 1)
                    nc.tensor.transpose(bZ[:, 384:384 + TOK], LTOK[:, :], IDN[:, :]).then_inc(t5_ps, 1)

            run(slot)(pe)

            pe.wait_ge(fws_ready, 1)
            nc.tensor.transpose(bank[7][:, 0:C], FWS[:, :], IDN[:, :]).then_inc(fwst_ps, 1)
            pe.wait_ge(fwst_sb, 1)
            
            def inputs(r, h):
                pe.wait_ge(lr_ld, 16 * (r + 1))
                mm(bank[h][:, :], FWST[:, :],
                   XR[:, :, :].rearrange("p a n -> p (a n)")[:, bass.ds((r & 1) * L + 512 * h, 512)],
                   start=True, stop=True, skip_group_check=True).then_inc(wx2_ps, 1)

            inputs(0, 0)

            def row(r, last_row):
                for w in range(WW):
                    h, t = w // 16, w % 16
                    pe.wait_ge(y2, WW * r + w + 1)
                    mm(bank[h][:, t * B:(t + 1) * B], VT[:, :], YS[:, (w - 1) % WW, :], start=False, stop=True,
                       skip_group_check=True).then_inc(pre2, 1)
                    if w == 2:
                        inputs(r, 1)
                    if w == 18 and not last_row:
                        inputs(r + 1, 0)

            with pe.Fori(0, HH - 1) as r:
                row(r, False)
            row(HH - 1, True)


def kernel(x, L0_conv_gamma, L0_conv_beta, L0_conv_w_in, L0_conv_b_in, L0_conv_w_ih, L0_conv_b_ih, L0_conv_w_hh,
           L0_conv_b_hh, L0_conv_w_out, L0_conv_b_out, L0_ffn_router_w, L0_ffn_router_b, L0_ffn_expert_w,
           L0_ffn_expert_b, L1_conv_kernel, L1_conv_bias, L1_ffn_W, L1_ffn_V, L1_ffn_gamma, L1_ffn_beta):
    import numpy as np
    import concourse.bacc as bacc
    from concourse.bass_utils import run_bass_kernel_spmd

    def parts(w):
        w = np.asarray(w)
        return w.reshape(-1, 128, w.shape[-1]).transpose(1, 0, 2)

    def col(v):
        return np.asarray(v).reshape(-1, 128).T

    def row(v):
        return np.asarray(v).reshape(1, -1)

    ins = dict(
        x=np.asarray(x).reshape(B, C, L),
        w_inT=np.asarray(L0_conv_w_in).T, b_in=col(L0_conv_b_in),
        w_ihT=parts(np.asarray(L0_conv_w_ih).T), b_ih=row(L0_conv_b_ih),
        w_hhT=parts(np.asarray(L0_conv_w_hh).T), b_hh=row(L0_conv_b_hh),
        w_outT=parts(np.asarray(L0_conv_w_out).T), b_out=col(L0_conv_b_out),
        gamma0=col(L0_conv_gamma), beta0=col(L0_conv_beta),
        router_w=np.asarray(L0_ffn_router_w), router_b=np.asarray(L0_ffn_router_b),
        expert_w=np.asarray(L0_ffn_expert_w).transpose(1, 0, 2).reshape(C, NE * C), expert_b=np.asarray(L0_ffn_expert_b),
        conv_w=np.asarray(L1_conv_kernel).reshape(C, TAPS * C), conv_b=col(L1_conv_bias),
        ffn_w=np.asarray(L1_ffn_W), ffn_vT=np.asarray(L1_ffn_V).T,
        gamma1=col(L1_ffn_gamma), beta1=col(L1_ffn_beta))
    nc = bacc.Bacc("TRN2", target_bir_lowering=False, num_devices=1)
    arrays, args = {}, {}
    for name, a in ins.items():
        a = np.ascontiguousarray(a)
        arrays[f"in_{name}"] = a
        args[name] = nc.dram_tensor(f"in_{name}", a.shape, mybir.dt.from_np(a.dtype), kind="ExternalInput").ap()
    lt_rows = nc.dram_tensor("lt_rows", (HH, C, L), F32).ap()
    out = nc.dram_tensor("out", (B, C, L), F32, kind="ExternalOutput").ap()
    metaformer(nc, **args, lt_rows=lt_rows, out=out)
    r = run_bass_kernel_spmd(nc, [arrays], core_ids=[0])
    return r.results[0]["out"].reshape(B, C, HH, WW)
```

```python
import concourse.bass as bass
from concourse import mybir
from contextlib import ExitStack

F32 = mybir.dt.float32
BF16 = mybir.dt.bfloat16
U32 = mybir.dt.uint32
ALU = mybir.AluOpType
ACT = mybir.ActivationFunctionType

B, C, HH, WW = 32, 128, 32, 32
L = HH * WW
STEPS = 4
TOK = STEPS * B
GROUPS = L // STEPS
PER_ROW = WW // STEPS
IMGS = B // PER_ROW
RIN, RH = 256, 512
KI, KH = RIN // 128, RH // 128
NE = 8
TAPS, PAD = 9, 4
EPS_C, EPS_T, EPS_BN = 1e-6, 1e-5, 1e-5

LAG = dict(z=0, rnn=1, moe=2, put=3, conv=PER_ROW + 3, ln=PER_ROW + 4, wx=PER_ROW + 5)


def stages_in(slot):
    return frozenset(s for s, lag in LAG.items() if 0 <= slot - lag < GROUPS)


def segments():
    pairs = (GROUPS + max(LAG.values()) + 1) // 2
    kind = [(stages_in(2 * p), stages_in(2 * p + 1), stages_in(2 * p + 2)) for p in range(pairs)]
    out = []
    for p in range(pairs):
        if out and kind[p] == kind[out[-1][0]]:
            out[-1][1] += 1
        else:
            out.append([p, 1])
    return [tuple(x) for x in out]


def metaformer(nc, x, w_inT, b_in, w_ihT, b_ih, w_hhT, b_hh, w_outT, b_out, gamma0, beta0,
               router_w, router_b, expert_w, expert_b, conv_w, conv_b, ffn_w, ffn_vT, gamma1, beta1,
               lt_rows, out):
    ctx = ExitStack()
    with ctx:
        def sb(name, shape, dt=F32):
            return ctx.enter_context(nc.sbuf_tensor(name, shape, dt))

        def sem(name):
            return ctx.enter_context(nc.semaphore(name))

        X = sb("X", [128, B, L])
        XR = sb("XR", [128, 2, L])
        LROW = sb("LROW", [128, 2, WW, B])
        CI = sb("CI", [128, 2, B, WW])
        Y = sb("Y", [128, B, WW])
        WHH = sb("WHH", [128, KH, RH])
        WIH = sb("WIH", [128, KI, RH])
        WIN = sb("WIN", [128, RIN])
        WINS = sb("WINS", [128, RIN])
        WOUT = sb("WOUT", [128, KH, C])
        EW = sb("EW", [128, NE * C])
        RW = sb("RW", [128, NE])
        RWC = sb("RWC", [128, NE])
        CW = sb("CW", [128, TAPS * C])
        FW = sb("FW", [128, C])
        FWT = sb("FWT", [128, C])
        VT = sb("VT", [128, C])
        EB = sb("EB", [NE, C])
        RB = sb("RB", [128, NE])
        BIN = sb("BIN", [128, KI])
        ZB = sb("ZB", [128, KI])
        BOUT = sb("BOUT", [128, 1])
        CB = sb("CB", [128, 1])
        G0, B0, G1, B1 = (sb(n, [128, 1]) for n in ("G0", "B0", "G1", "B1"))
        BX = sb("BX", [3 * KH, 128], BF16)
        SEL = sb("SEL", [3 * KH, KH * B], BF16)
        IDN = sb("IDN", [128, 128])
        STX = sb("STX", [128, 2, 4, 6])
        MVX = sb("MVX", [128, 4, 4, 2])
        VX, RX, NX = (sb(n, [128, 4, 4]) for n in ("VX", "RX", "NX"))
        CEN = sb("CEN", [128, 128])
        IOTA = sb("IOTA", [128, NE])
        NHALF = sb("NHALF", [128, 4])
        WXS = sb("WXS", [128, GROUPS, 6])
        MV0 = sb("MV0", [128, 2])
        MV4 = sb("MV4", [128, 2])
        R0 = sb("R0", [128, 1])
        R4 = sb("R4", [128, 1])
        SC0, SH0, SC1, SH1, TMP0, TMP1 = (sb(n, [128, 1]) for n in ("SC0", "SH0", "SC1", "SH1", "TMP0", "TMP1"))
        XIN = sb("XIN", [128, 2, TOK])
        TH = sb("TH", [128, KI, TOK])
        INP = sb("INP", [128, 2, KI, TOK])
        HTOK = sb("HTOK", [128, 128])
        H = sb("H", [128, 2, KH, STEPS, B])
        TC = sb("TC", [128, TOK])
        ACC = sb("ACC", [128, C])
        ACC2 = sb("ACC2", [128, C])
        XLT = sb("XLT", [128, C])
        LTOK = sb("LTOK", [128, C])
        T3C = sb("T3C", [128, TOK])
        LC = sb("LC", [128, TOK])
        CC = sb("CC", [128, IMGS, WW + 2 * PAD])
        GP = sb("GP", [128, 128])
        GR = sb("GR", [128, NE])
        GA = sb("GA", [128, NE])
        GB = sb("GB", [128, NE])
        GT = sb("GT", [NE, TOK])
        LG = sb("LG", [128, NE])
        MX = sb("MX", [128, 8])
        IX = sb("IX", [128, 8], U32)
        IXF = sb("IXF", [128, 8])
        EX, DN, G_1, G_2 = (sb(n, [128, 1]) for n in ("EX", "DN", "G_1", "G_2"))
        ST1, ST2, ST3 = (sb(n, [128, 6]) for n in ("ST1", "ST2", "ST3"))
        MV1, MV2, MV3 = (sb(n, [128, 2]) for n in ("MV1", "MV2", "MV3"))
        V1, V2, V3, V0, V4 = (sb(n, [128, 1]) for n in ("V1", "V2", "V3", "V0", "V4"))
        R1, R2, R3 = (sb(n, [128, 1]) for n in ("R1", "R2", "R3"))

        bank = [ctx.enter_context(nc.psum_tensor(f"bank{i}", [128, 512], F32)) for i in range(8)]
        bPRE = bank[0:2]
        EPS_BANKS = [bank[2], bank[3]]
        bZ, bC, bT, bM = bank[4], bank[5], bank[6], bank[7]

        WXSF = WXS[:, :, :].rearrange("p t s -> p (t s)")
        BR = WXSF[0:1, 0:2 * RH].rearrange("p (a n) -> p a n", a=2)
        BHI = WXSF[0:1, 1024:1280].bitcast(BF16)
        BMID = WXSF[0:1, 1280:1536].bitcast(BF16)
        BLO = TH[0:1, :, :].rearrange("p k n -> p (k n)").bitcast(BF16)
        STAT0 = H[:, 0, :, :, :].rearrange("p k s b -> p (k s b)")[:, 0:64 * 6].rearrange("p (t s) -> p t s", s=6)
        FWS, FWST = T3C, LC
        XS = CI[:, :, :, :].rearrange("p a b w -> p (a b w)").rearrange("p (u n) -> p u n", u=4)
        XT = LROW[:, :, :, :].rearrange("p a w b -> p (a w b)").rearrange("p (u n) -> p u n", u=4)
        EWRAW = Y[:, :, :].rearrange("p b w -> p (b w)")
        XF = X[:, :, :].rearrange("p b l -> p (b l)")
        YS = Y[:, :, :].rearrange("p b w -> p (b w)").rearrange("p (w b) -> p w b", w=WW)

        x_ld = [sem(f"x_ld{i}") for i in range(4)]
        w_ld = sem("w_ld")
        b3_ld = sem("b3_ld")
        consts = sem("consts")
        pool_own, dve_own = sem("pool_own"), sem("dve_own")
        (tin_ps, mvx_ready, rx_ready, xt_ready, tout_ps, x_ready, norm_done, ewc_ps, ewc_sb, mv0_ready, r0_ready, zb_ps, sh0_ready,
         zb_ready, ys_zero, fwt_ps, fwt_sb) = (sem(n) for n in (
             "tin_ps", "mvx_ready", "rx_ready", "xt_ready", "tout_ps", "x_ready", "norm_done", "ewc_ps", "ewc_sb", "mv0_ready", "r0_ready",
             "zb_ps", "sh0_ready", "zb_ready", "ys_zero", "fwt_ps", "fwt_sb"))
        b_split, b_rows = sem("b_split"), sem("b_rows")
        (xin_ready, z_ps, th_ready, inp_ready, pre_ready, tanh_done, ht_ps, h_sb, o_ps, tc_ready, t1_ps, rt_ps, moe_ps,
         mv1_ready, r1_ready, mx_ready, e_ready, g_ready, gt_ps, gt_sb, acc_ps, acc_sb, comb_done, mv2_ready,
         r2_ready, xlt_ready, t23_ps, xl_sb, cc_ready, conv_ps, y_ready, t3c_ready, t4_ps, mv3_ready, r3_ready,
         l_tok, t5_ps, lc_sb, wx_ps, wxs, lrow, spilled, xr_ld) = (sem(n) for n in (
             "xin_ready", "z_ps", "th_ready", "inp_ready", "pre_ready", "tanh_done", "ht_ps", "h_sb", "o_ps", "tc_ready", "t1_ps",
             "rt_ps", "moe_ps", "mv1_ready", "r1_ready", "mx_ready", "e_ready", "g_ready", "gt_ps", "gt_sb",
             "acc_ps", "acc_sb", "comb_done", "mv2_ready", "r2_ready", "xlt_ready", "t23_ps", "xl_sb", "cc_ready",
             "conv_ps", "y_ready", "t3c_ready", "t4_ps", "mv3_ready", "r3_ready", "l_tok", "t5_ps", "lc_sb",
             "wx_ps", "wxs", "lrow", "spilled", "xr_ld"))
        (mv4_ready, r4_ready, fws_ready, fwst_ps, fwst_sb, lr_ld, wx2_ps, pre2, y2, added, stored) = (
            sem(n) for n in ("mv4_ready", "r4_ready", "fws_ready", "fwst_ps", "fwst_sb", "lr_ld", "wx2_ps", "pre2",
                             "y2", "added", "stored"))

        stx = sem("stx")
        (pv1, pv2, pv3, x3_ready, comb, st1, st2, st3, lg, gate, gr_ready, px1, px2) = (sem(n) for n in (
            "pv1", "pv2", "pv3", "x3_ready", "comb", "st1", "st2", "st3", "lg", "gate", "gr_ready", "px1", "px2"))

        SEGS = segments()
        MARGIN = 3 * B
        weights = [(WHH[:, :, :], w_hhT), (WIH[:, :, :], w_ihT), (WIN[:, :], w_inT), (WOUT[:, :, :], w_outT),
                   (EWRAW, expert_w), (RW[:, :], router_w), (CW[:, :], conv_w), (FW[:, :], ffn_w), (VT[:, :], ffn_vT),
                   (EB[:, :], expert_b), (BIN[:, :], b_in), (BOUT[:, :], b_out), (CB[:, :], conv_b),
                   (G0[:, :], gamma0), (B0[:, :], beta0), (G1[:, :], gamma1), (B1[:, :], beta1),
                   (BR[:, 0, :], b_ih), (BR[:, 1, :], b_hh), (RB[:, :], router_b.partition_broadcast(128))]
        W_LD = 16 * len(weights)

        sp_waits, pool_waits, dve_waits = sem("sp_waits"), sem("pool_waits"), sem("dve_waits")

        def wait_first(eng, s, value, count):
            eng.wait_ge(s, value)
            eng.sem_inc(count, 1)

        block = ctx.enter_context(nc.Block())

        def run(body):
            def over(eng):
                for p0, n in SEGS:
                    def pair(p, base):
                        for s in (0, 1):
                            body(p * 2 + s, s, stages_in(base + s), stages_in(base + s + 1))
                    if n == 1:
                        pair(p0, 2 * p0)
                    else:
                        with eng.Fori(p0, p0 + n) as p:
                            pair(p, 2 * p0)
            return over

        @block.sync
        def _(sp):
            def x_chunk(k, u, first=False):
                if not first:
                    wait_first(sp, tin_ps, (k - 1) * 4 + u + 1, sp_waits)
                sp.dma_start(XS[:, u, :], x[bass.ds((k & 15) * 2 + u // 2, 1), :, 512 * (u % 2):512 * (u % 2) + 512
                                            ].rearrange("b c l -> (b c) l")).then_inc(x_ld[u], 16)

            for u in range(4):
                x_chunk(0, u, first=True)
            with sp.Fori(1, 16) as k:
                for u in range(4):
                    x_chunk(k, u)

            def some_row(r):
                return r & (HH - 1)

            def xr_load(r):
                wait_first(sp, xr_ld, 16 * r, sp_waits)
                sp.dma_start(xr_row(r), x_row(r)).then_inc(xr_ld, 16)

            def xr_row(r):
                return XR[:, bass.ds(r & 1, 1), :].rearrange("p a (b w) -> p (a b) w", b=B)

            def x_row(r):
                return x[:, :, bass.ds(some_row(r) * WW, WW)].rearrange("b c w -> c b w")

            def spill(r):
                wait_first(sp, lrow, PER_ROW * (r + 1), sp_waits)
                wait_first(sp, spilled, 16 * (r + 2), sp_waits)
                sp.dma_start(lt_rows[bass.ds(some_row(r), 1), :, :].rearrange("r c n -> (r c) n"),
                             LROW[:, bass.ds(r & 1, 1), :, :].rearrange("p a w b -> p (a w b)")).then_inc(spilled, 16)

            for r in range(4):
                if r >= 2:
                    wait_first(sp, tc_ready, PER_ROW * (r - 1), sp_waits)
                xr_load(r)
            with sp.Fori(0, HH - 4) as r:
                spill(r)
                wait_first(sp, tc_ready, PER_ROW * (r + 3), sp_waits)
                xr_load(r + 4)
            for r in range(HH - 4, HH):
                spill(r)
                if r == HH - 4:
                    wait_first(sp, tc_ready, GROUPS, sp_waits)
            wait_first(sp, spilled, 16 * (HH + 2), sp_waits)

            def lr_load(r):
                wait_first(sp, lr_ld, 16 * r, sp_waits)
                sp.dma_start(XR[:, bass.ds(r & 1, 1), :].rearrange("p a n -> p (a n)"),
                             lt_rows[bass.ds(some_row(r), 1), :, :].rearrange("r c n -> (r c) n")).then_inc(lr_ld, 16)
            lr_load(0)
            lr_load(1)

            def four_rows(q, loads):
                for u in range(loads):
                    wait_first(sp, wx2_ps, 16 * q + 4 * u + 4, sp_waits)
                    lr_load(q * 4 + u + 2)
                wait_first(sp, added, 8 * q + 8, sp_waits)
                sp.dma_start(out[:, :, bass.ds((q & 7) * 4 * WW, 4 * WW)].rearrange("b c l -> c b l"),
                             X[:, :, bass.ds((q & 7) * 4 * WW, 4 * WW)]).then_inc(stored, 16)
            with sp.Fori(0, HH // 4 - 1) as q:
                four_rows(q, 4)
            four_rows(HH // 4 - 1, 2)
            wait_first(sp, stored, 16 * (HH // 4), sp_waits)

        @block.gpsimd
        def _(pool):
            own = [0]

            def link(ins):
                own[0] += 1
                ins.then_inc(pool_own, 1)
                pool.wait_ge(pool_own, own[0])

            link(nc.gpsimd.memset(IDN[:, :], 0.0))
            nc.gpsimd.affine_select(out=IDN[:, :], in_=IDN[:, :], compare_op=ALU.not_equal, fill=1.0, base=0,
                                    pattern=[[-1, 128]], channel_multiplier=1).then_inc(consts, 1)
            pool.wait_ge(consts, 1)
            nc.gpsimd.tensor_scalar(CEN[:, :], IDN[:, :], -1.0 / C, None, ALU.add).then_inc(consts, 1)
            for e in range(NE):
                nc.gpsimd.memset(IOTA[:, e:e + 1], float(e)).then_inc(consts, 1)
            link(nc.gpsimd.memset(SEL[:, :], 1.0))
            link(nc.gpsimd.affine_select(out=SEL[:, :], in_=SEL[:, :], compare_op=ALU.is_ge, fill=0.0, base=0,
                                         pattern=[[-3, KH], [0, B]], channel_multiplier=1))
            nc.gpsimd.affine_select(out=SEL[:, :], in_=SEL[:, :], compare_op=ALU.is_ge, fill=0.0, base=2,
                                    pattern=[[3, KH], [0, B]], channel_multiplier=-1).then_inc(consts, 1)
            nc.gpsimd.memset(CC[:, :, :], 0.0).then_inc(consts, 1)
            nc.gpsimd.memset(GP[:, :], 0.0).then_inc(consts, 1)
            nc.gpsimd.memset(H[:, 1, :, :, :], 0.0).then_inc(consts, 1)
            link(nc.gpsimd.memset(NHALF[:, :], -0.5))

            def rstd(r, v, mv, eps, ready):
                link(nc.gpsimd.tensor_scalar(v[:, :], mv[:, 1:2], eps, None, ALU.add))
                nc.gpsimd.tensor_tensor(r[:, :], v[:, :], NHALF[:, 0:1], ALU.pow).then_inc(ready, 1)

            with pool.Fori(0, 16) as k:
                for u in range(4):
                    t = k * 4 + u
                    wait_first(pool, mvx_ready, t + 1, pool_waits)
                    nc.gpsimd.tensor_scalar(VX[:, u, :], MVX[:, u, :, 1], EPS_C, None, ALU.add).then_inc(px1, 1)
                    pool.wait_ge(px1, t + 1)
                    nc.gpsimd.tensor_tensor(RX[:, u, :], VX[:, u, :], NHALF[:, :], ALU.pow).then_inc(px2, 1)
                    pool.wait_ge(px2, 2 * t + 1)
                    nc.gpsimd.tensor_tensor(VX[:, u, :], MVX[:, u, :, 0], RX[:, u, :], ALU.mult).then_inc(px2, 1)
                    wait_first(pool, px2, 2 * t + 2, pool_waits)
                    nc.gpsimd.tensor_scalar(NX[:, u, :], VX[:, u, :], -1.0, None, ALU.mult).then_inc(rx_ready, 1)

            pool.wait_ge(ewc_sb, 3)
            nc.gpsimd.memset(Y[:, :, :], 0.0).then_inc(ys_zero, 1)
            nc.gpsimd.memset(V3[:, :], 0.0).then_inc(spilled, 16)
            nc.gpsimd.memset(V2[:, :], 0.0).then_inc(spilled, 16)
            pool.wait_ge(mv0_ready, 1)
            rstd(R0, V0, MV0, EPS_BN, r0_ready)

            def gather(i, s):
                nc.gpsimd.tensor_copy(XIN[:, s, :].rearrange("p (s b) -> p s b", s=STEPS),
                                      X[:, :, bass.ds((i & (GROUPS - 1)) * STEPS, STEPS)].rearrange("p b s -> p s b")
                                      ).then_inc(xin_ready, 1)

            pool.wait_ge(norm_done, 64)
            gather(0, 0)

            pool.wait_ge(ys_zero, 1)

            def slot(i, s, on, nxt):
                q, l, n, o = i - LAG["conv"], i - LAG["ln"], i - LAG["put"], i - LAG["moe"]
                if "conv" in on:
                    if "put" in on:
                        pool.wait_ge(xl_sb, n)
                    else:
                        pool.wait_ge(xl_sb, GROUPS)
                    pool.wait_ge(conv_ps, q)
                    pool.wait_ge(y_ready, q)
                    b0 = (q & (PER_ROW - 1)) * IMGS
                    row = (q >> 3) & (HH - 1)
                    nc.gpsimd.tensor_tensor(
                        CC[:, :, PAD:PAD + WW],
                        CI[:, :, :, :].rearrange("p a b w -> p (a b) w")[:, bass.ds((row & 1) * B + b0, IMGS), :],
                        Y[:, bass.ds(b0, IMGS), :], ALU.add).then_inc(cc_ready, 1)
                if "z" in nxt:
                    wait_first(pool, z_ps, i, pool_waits)
                    gather(i + 1, 1 - s)
                if "ln" in on:
                    wait_first(pool, mv3_ready, l + 1, pool_waits)
                    nc.gpsimd.tensor_scalar(V3[:, :], MV3[:, 1:2], EPS_T, None, ALU.add).then_inc(pv3, 1)
                    pool.wait_ge(pv3, l + 1)
                    nc.gpsimd.tensor_tensor(R3[:, :], V3[:, :], NHALF[:, 0:1], ALU.pow).then_inc(r3_ready, 1)
                if "put" in on:
                    wait_first(pool, mv2_ready, n + 1, pool_waits)
                    nc.gpsimd.tensor_scalar(V2[:, :], MV2[:, 1:2], EPS_C, None, ALU.add).then_inc(pv2, 1)
                    pool.wait_ge(pv2, n + 1)
                    nc.gpsimd.tensor_tensor(R2[:, :], V2[:, :], NHALF[:, 0:1], ALU.pow).then_inc(r2_ready, 1)
                if "moe" in on:
                    wait_first(pool, mv1_ready, o + 1, pool_waits)
                    nc.gpsimd.tensor_scalar(V1[:, :], MV1[:, 1:2], EPS_T, None, ALU.add).then_inc(pv1, 1)
                    pool.wait_ge(pv1, o + 1)
                    nc.gpsimd.tensor_tensor(R1[:, :], V1[:, :], NHALF[:, 0:1], ALU.pow).then_inc(r1_ready, 1)
                if "conv" in on:
                    pool.wait_ge(y_ready, q + 1)
                    pool.wait_ge(t4_ps, q)
                    b0 = (q & (PER_ROW - 1)) * IMGS
                    row = (q >> 3) & (HH - 1)
                    here = X[:, bass.ds(b0, IMGS), bass.ds(row * WW, WW)]
                    t3 = T3C[:, :].rearrange("p (b w) -> p b w", b=IMGS)
                    nc.gpsimd.tensor_tensor(t3, here, Y[:, bass.ds(b0, IMGS), :], ALU.add).then_inc(t3c_ready, 1)
                    wait_first(pool, t3c_ready, q + 1, pool_waits)
                    nc.gpsimd.tensor_copy(here, t3).then_inc(x3_ready, 1)
                if "ln" in on:
                    pool.wait_ge(lc_sb, l + 1)
                    row = (l >> 3) & (HH - 1)
                    wait_first(pool, spilled, 16 * row + 16, pool_waits)
                    nc.gpsimd.tensor_copy(
                        LROW[:, :, :, :].rearrange("p a w b -> p (a w) b")[
                            :, bass.ds((row & 1) * WW, WW), bass.ds((l & (PER_ROW - 1)) * IMGS, IMGS)],
                        LC[:, :].rearrange("p (b w) -> p w b", b=IMGS)).then_inc(lrow, 1)

            run(slot)(pool)
            pool.wait_ge(x3_ready, GROUPS)
            nc.gpsimd.memset(YS[:, WW - 1, :], 0.0).then_inc(y2, 1)
            pool.wait_ge(mv4_ready, 1)
            rstd(R4, V4, MV4, EPS_BN, r4_ready)

        @block.scalar
        def _(act):
            for dst, src in weights:
                act.dma_start(dst, src).then_inc(w_ld, 16)

            with act.Fori(0, 16) as k:
                def normed(u):
                    act.wait_ge(rx_ready, k * 4 + u + 1)
                    for j in range(4):
                        last = nc.scalar.activation(XT[:, u, j * 128:(j + 1) * 128], bank[u][:, j * 128:(j + 1) * 128],
                                                    ACT.Identity, scale=RX[:, u, j:j + 1], bias=NX[:, u, j:j + 1])
                    last.then_inc(xt_ready, 1)

                def evict(u):
                    act.wait_ge(tout_ps, k * 4 + u + 1)
                    nc.scalar.copy(XF[:, bass.ds(((k & 15) * 4 + u) * 512, 512)], bank[4 + u][:, :]).then_inc(x_ready, 1)
                normed(0)
                normed(1)
                evict(0)
                normed(2)
                evict(1)
                normed(3)
                evict(2)
                evict(3)
            act.wait_ge(b_split, 1)
            for j in range(KH):
                for part, src in enumerate((BHI, BMID, BLO)):
                    act.dma_start(BX[3 * j + part:3 * j + part + 1, :], src[:, j * 128:(j + 1) * 128]).then_inc(b_rows, 16)

            def slot(i, s, on, nxt):
                g, o, n, q, l = i - 1, i - LAG["moe"], i - LAG["put"], i - LAG["conv"], i - LAG["ln"]

                def step(t):
                    if "rnn" in on:
                        act.wait_ge(pre_ready, STEPS * g + t + 1)
                        nc.scalar.activation(HTOK[:, :], bPRE[t % 2][:, 0:128], ACT.Tanh).then_inc(tanh_done, 1)
                        act.wait_ge(ht_ps, STEPS * g + t + 1)
                        nc.scalar.copy(H[:, 1 - s, :, t, :], bPRE[t % 2][:, 128:256].rearrange("p (k b) -> p k b", k=KH)
                                       ).then_inc(h_sb, 1)
                step(0)
                if "put" in on:
                    act.wait_ge(acc_ps, n + 1)
                    act.wait_ge(t23_ps, n)
                    nc.scalar.copy(ACC[:, :], bT[:, 0:C]).then_inc(acc_sb, 1)
                if "z" in on:
                    act.wait_ge(z_ps, i + 1)
                    act.wait_ge(inp_ready, i)
                    for k in range(KI):
                        last = nc.scalar.activation(TH[:, k, :], bZ[:, k * TOK:(k + 1) * TOK], ACT.Tanh,
                                                    bias=ZB[:, k:k + 1])
                    last.then_inc(th_ready, 1)
                step(1)
                step(2)
                if "conv" in on:
                    act.wait_ge(conv_ps, q + 1)
                    nc.scalar.activation(Y[:, bass.ds((q & (PER_ROW - 1)) * IMGS, IMGS), :],
                                         bC[:, 0:TOK].rearrange("p (b w) -> p b w", b=IMGS), ACT.Relu,
                                         bias=CB[:, 0:1]).then_inc(y_ready, 1)
                if "moe" in on:
                    act.wait_ge(mx_ready, o + 1)
                    nc.scalar.activation(EX[:, :], MX[:, 0:1], ACT.Exp, scale=-1.0, bias=MX[:, 1:2]).then_inc(e_ready, 1)
                step(3)
                if "put" in on:
                    act.wait_ge(t23_ps, n + 1)
                    nc.scalar.copy(X[:, :, bass.ds((n & (GROUPS - 1)) * STEPS, STEPS)].rearrange("p b s -> p s b"),
                                   bC[:, 0:TOK].rearrange("p (s b) -> p s b", s=STEPS))
                    nc.scalar.copy(
                        CI[:, :, :, :].rearrange("p a b w -> p (a b) w")[
                            :, bass.ds(((n >> 3) & 1) * B, B), bass.ds((n & (PER_ROW - 1)) * STEPS, STEPS)
                        ].rearrange("p b s -> p s b"),
                        bC[:, TOK:2 * TOK].rearrange("p (s b) -> p s b", s=STEPS)).then_inc(xl_sb, 1)
                if "moe" in on:
                    act.wait_ge(gt_ps, o + 1)
                    nc.scalar.copy(GT[:, :], bM[0:NE, 256:256 + TOK]).then_inc(gt_sb, 1)
                if "ln" in on:
                    act.wait_ge(t5_ps, l + 1)
                    if "wx" in on:
                        act.wait_ge(wx_ps, l)
                        act.wait_ge(lrow, l)
                    nc.scalar.copy(LC[:, :], bC[:, 2 * C:3 * C]).then_inc(lc_sb, 1)

            run(slot)(act)

            act.wait_ge(fwst_sb, 1)

            def row(r, first=False):
                for w in range(WW):
                    if w % 16 == 15 and not (first and w == 15):
                        act.wait_ge(added, 2 * r + w // 16)
                    act.wait_ge(pre2, WW * r + w + 1)
                    at = MARGIN + (w % 8) * B
                    nc.scalar.activation(YS[:, w, :], bank[w // 8][:, at:at + B], ACT.Sigmoid, bias=SH1[:, 0:1]
                                         ).then_inc(y2, 1)

            row(0, first=True)
            with act.Fori(1, HH) as r:
                row(r)

        @block.vector
        def _(dve):
            own = [0]

            def link(ins):
                own[0] += 1
                ins.then_inc(dve_own, 1)
                dve.wait_ge(dve_own, own[0])

            dve.wait_ge(w_ld, W_LD)
            link(nc.vector.tensor_tensor(BR[:, 0, :], BR[:, 0, :], BR[:, 1, :], ALU.add))
            link(nc.vector.tensor_copy(BHI[:, :], BR[:, 0, :]))
            link(nc.vector.tensor_tensor(BR[:, 1, :], BR[:, 0, :], BHI[:, :], ALU.subtract))
            link(nc.vector.tensor_copy(BMID[:, :], BR[:, 1, :]))
            link(nc.vector.tensor_tensor(BR[:, 0, :], BR[:, 1, :], BMID[:, :], ALU.subtract))
            nc.vector.tensor_copy(BLO[:, :], BR[:, 0, :]).then_inc(b_split, 1)
            with dve.Fori(0, 16) as k:
                def over_channels(u):
                    dve.wait_ge(tin_ps, k * 4 + u + 1)
                    for j in range(4):
                        last = nc.vector.bn_stats(STX[:, u % 2, j, :], bank[u][:, j * 128:(j + 1) * 128])
                    last.then_inc(stx, 1)
                    wait_first(dve, stx, k * 4 + u + 1, dve_waits)
                    for j in range(4):
                        last = nc.vector.bn_aggr(MVX[:, u, j, :], STX[:, u % 2, j, :])
                    last.then_inc(mvx_ready, 1)

                def over_tokens(u):
                    t = (k & 15) * 4 + u
                    dve.wait_ge(x_ready, k * 4 + u + 1)
                    nc.vector.bn_stats(STAT0[:, bass.ds(t, 1), :].rearrange("p t s -> p (t s)"),
                                       XF[:, bass.ds(t * 512, 512)]).then_inc(norm_done, 1)
                over_channels(0)
                over_channels(1)
                over_tokens(0)
                over_channels(2)
                over_tokens(1)
                over_channels(3)
                over_tokens(2)
                over_tokens(3)
            dve.wait_ge(ewc_ps, 1)
            nc.vector.tensor_copy(EW[:, 0:512], bank[0][:, :]).then_inc(ewc_sb, 1)
            dve.wait_ge(ewc_ps, 2)
            nc.vector.tensor_copy(EW[:, 512:1024], bank[1][:, :]).then_inc(ewc_sb, 1)
            dve.wait_ge(ewc_ps, 3)
            nc.vector.tensor_copy(RWC[:, :], bank[2][:, 0:NE]).then_inc(ewc_sb, 1)
            dve.wait_ge(ewc_ps, 4)
            nc.vector.tensor_copy(FWT[:, :], bank[3][:, 0:C]).then_inc(ewc_sb, 1)

            dve.wait_ge(norm_done, 64)
            nc.vector.bn_aggr(MV0[:, :], STAT0[:, :, :].rearrange("p t s -> p (t s)")).then_inc(mv0_ready, 1)
            dve.wait_ge(r0_ready, 1)
            link(nc.vector.tensor_tensor(SC0[:, :], G0[:, :], R0[:, :], ALU.mult))
            nc.vector.tensor_scalar(WINS[:, :], WIN[:, :], SC0[:, 0:1], None, ALU.mult)
            link(nc.vector.tensor_tensor(TMP0[:, :], MV0[:, 0:1], SC0[:, :], ALU.mult))
            nc.vector.tensor_tensor(SH0[:, :], B0[:, :], TMP0[:, :], ALU.subtract).then_inc(sh0_ready, 1)
            dve.wait_ge(zb_ps, 1)
            nc.vector.tensor_tensor(ZB[:, :], bank[7][:, 0:KI], BIN[:, :], ALU.add).then_inc(zb_ready, 1)
            dve.wait_ge(consts, 14)

            def slot(i, s, on, nxt):
                o, n, l, w = i - LAG["moe"], i - LAG["put"], i - LAG["ln"], i - LAG["wx"]
                if "moe" in on:
                    dve.wait_ge(o_ps, o + 1)
                    dve.wait_ge(xr_ld, 16 * ((o >> 3) + 1))
                    dve.wait_ge(moe_ps, o)
                    src = XR[:, :, :].rearrange("p a (b w) -> p (a b) w", b=B)[
                        :, bass.ds(((o >> 3) & 1) * B, B), bass.ds((o & (PER_ROW - 1)) * STEPS, STEPS)]
                    nc.vector.scalar_tensor_tensor(
                        TC[:, :].rearrange("p (s b) -> p s b", s=STEPS), bM[:, 0:TOK].rearrange("p (s b) -> p s b", s=STEPS),
                        BOUT[:, 0:1], src.rearrange("p b s -> p s b"), ALU.add, ALU.add).then_inc(tc_ready, 1)
                if "z" in on:
                    dve.wait_ge(th_ready, i + 1)
                    for k in range(KI):
                        last = nc.vector.scalar_tensor_tensor(
                            INP[:, s, k, :], bZ[:, k * TOK:(k + 1) * TOK], ZB[:, k:k + 1], TH[:, k, :],
                            ALU.add, ALU.subtract)
                    last.then_inc(inp_ready, 1)
                def experts(es):
                    for e in es:
                        src = EPS_BANKS[e // 4][:, (e % 4) * C:(e % 4 + 1) * C]
                        acc = (ACC, ACC2)[e % 2]
                        if e >= 2:
                            dve.wait_ge(comb, NE * n + e - 1)
                        if e == 1:
                            ins = nc.vector.tensor_scalar(ACC2[:, :], src, GR[:, 1:2], None, ALU.mult)
                        else:
                            ins = nc.vector.scalar_tensor_tensor(acc[:, :], src, GR[:, e:e + 1], acc[:, :], ALU.mult, ALU.add)
                        ins.then_inc(comb, 1)

                if "put" in on:
                    dve.wait_ge(acc_sb, n + 1)
                    dve.wait_ge(moe_ps, n + 1)
                    experts(range(0, 3))
                if "ln" in on:
                    dve.wait_ge(t4_ps, l + 1)
                    nc.vector.bn_stats(ST3[:, :], bT[:, 256:256 + C]).then_inc(st3, 1)
                if "put" in on:
                    experts(range(3, 4))
                if "ln" in on:
                    wait_first(dve, st3, l + 1, dve_waits)
                    nc.vector.bn_aggr(MV3[:, :], ST3[:, :]).then_inc(mv3_ready, 1)
                if "put" in on:
                    experts(range(4, NE))
                    dve.wait_ge(comb, NE * n + NE)
                    nc.vector.tensor_tensor(ACC[:, :], ACC[:, :], ACC2[:, :], ALU.add).then_inc(comb_done, 1)
                if "ln" in on:
                    dve.wait_ge(r3_ready, l + 1)
                    nc.vector.tensor_scalar(LTOK[:, :], bT[:, 256:256 + C], MV3[:, 0:1], R3[:, 0:1],
                                            ALU.subtract, ALU.mult).then_inc(l_tok, 1)
                if "put" in on:
                    dve.wait_ge(comb_done, n + 1)
                    nc.vector.bn_stats(ST2[:, :], ACC[:, :]).then_inc(st2, 1)
                    wait_first(dve, st2, n + 1, dve_waits)
                    nc.vector.bn_aggr(MV2[:, :], ST2[:, :]).then_inc(mv2_ready, 1)
                if "moe" in on:
                    dve.wait_ge(t1_ps, o + 1)
                    nc.vector.bn_stats(ST1[:, :], bT[:, 0:C]).then_inc(st1, 1)
                    wait_first(dve, st1, o + 1, dve_waits)
                    nc.vector.bn_aggr(MV1[:, :], ST1[:, :]).then_inc(mv1_ready, 1)
                if "put" in on:
                    dve.wait_ge(r2_ready, n + 1)
                    nc.vector.tensor_scalar(XLT[:, :], ACC[:, :], MV2[:, 0:1], R2[:, 0:1], ALU.subtract, ALU.mult
                                            ).then_inc(xlt_ready, 1)
                if "moe" in on:
                    dve.wait_ge(rt_ps, o + 1)
                    dve.wait_ge(r1_ready, o + 1)
                    nc.vector.scalar_tensor_tensor(LG[:, :], bM[:, 128:128 + NE], R1[:, 0:1], RB[:, :],
                                                   ALU.mult, ALU.add).then_inc(lg, 1)
                    wait_first(dve, lg, o + 1, dve_waits)
                    nc.vector.max(MX[:, :], LG[:, :]).then_inc(mx_ready, 1)
                    wait_first(dve, mx_ready, o + 1, dve_waits)
                    nc.vector.max_index(IX[:, :], MX[:, :], LG[:, :]).then_inc(gate, 1)
                    dve.wait_ge(gate, 5 * o + 1)
                    dve.wait_ge(e_ready, o + 1)
                    nc.vector.tensor_copy(IXF[:, :], IX[:, :])
                    nc.vector.tensor_scalar(DN[:, :], EX[:, :], 1.0, None, ALU.add).then_inc(gate, 1)
                    dve.wait_ge(gate, 5 * o + 2)
                    nc.vector.reciprocal(G_1[:, :], DN[:, :]).then_inc(gate, 1)
                    dve.wait_ge(gate, 5 * o + 3)
                    nc.vector.tensor_tensor(G_2[:, :], EX[:, :], G_1[:, :], ALU.mult)
                    nc.vector.tensor_scalar(GA[:, :], IOTA[:, :], IXF[:, 0:1], G_1[:, 0:1], ALU.is_equal, ALU.mult
                                            ).then_inc(gate, 1)
                    dve.wait_ge(gate, 5 * o + 4)
                    nc.vector.tensor_scalar(GB[:, :], IOTA[:, :], IXF[:, 1:2], G_2[:, 0:1], ALU.is_equal, ALU.mult
                                            ).then_inc(gate, 1)
                    dve.wait_ge(gate, 5 * o + 5)
                    nc.vector.tensor_tensor(GP[:, 0:NE], GA[:, :], GB[:, :], ALU.add).then_inc(g_ready, 1)
                    dve.wait_ge(g_ready, o + 1)
                    nc.vector.tensor_scalar(GR[:, :], GP[:, 0:NE], R1[:, 0:1], None, ALU.mult).then_inc(gr_ready, 1)
                    dve.wait_ge(gr_ready, o + 1)
                if "wx" in on:
                    dve.wait_ge(wx_ps, w + 1)
                    nc.vector.bn_stats(WXS[:, bass.ds(w & (GROUPS - 1), 1), :].rearrange("p t s -> p (t s)"), bZ[:, 256:256 + TOK]
                                       ).then_inc(wxs, 1)

            run(slot)(dve)
            dve.wait_ge(wxs, GROUPS)
            nc.vector.bn_aggr(MV4[:, :], WXS[:, :, :].rearrange("p t s -> p (t s)")).then_inc(mv4_ready, 1)
            dve.wait_ge(r4_ready, 1)
            link(nc.vector.tensor_tensor(SC1[:, :], G1[:, :], R4[:, :], ALU.mult))
            nc.vector.tensor_scalar(FWS[:, :], FW[:, :], SC1[:, 0:1], None, ALU.mult).then_inc(fws_ready, 1)
            link(nc.vector.tensor_tensor(TMP1[:, :], MV4[:, 0:1], SC1[:, :], ALU.mult))
            link(nc.vector.tensor_tensor(SH1[:, :], B1[:, :], TMP1[:, :], ALU.subtract))
            dve.wait_ge(fwst_ps, 1)
            nc.vector.tensor_copy(FWST[:, :], bank[7][:, 0:C]).then_inc(fwst_sb, 1)

            with dve.Fori(0, HH) as r:
                for h in range(2):
                    dve.wait_ge(y2, WW * r + 16 * (h + 1) + 1)
                    here = X[:, :, bass.ds((r & (HH - 1)) * WW + 16 * h, 16)]
                    nc.vector.tensor_tensor(here, here, YS[:, 16 * h:16 * h + 16, :].rearrange("p w b -> p b w"),
                                            ALU.add).then_inc(added, 1)

        @block.tensor
        def _(pe):
            mm = nc.tensor.matmul
            pe.wait_ge(consts, 1)

            def four(k, first=False):
                def tokens(u):
                    pe.wait_ge(x_ld[u], 16 * (k + 1))
                    if not first:
                        pe.wait_ge(xt_ready, (k - 1) * 4 + u + 1)
                    for j in range(4):
                        last = nc.tensor.transpose(bank[u][:, j * 128:(j + 1) * 128], XS[:, u, j * 128:(j + 1) * 128],
                                                   IDN[:, :])
                    last.then_inc(tin_ps, 1)

                def channels(u):
                    pe.wait_ge(xt_ready, k * 4 + u + 1)
                    if not first:
                        pe.wait_ge(x_ready, (k - 1) * 4 + u + 1)
                    for j in range(4):
                        last = nc.tensor.transpose(bank[4 + u][:, j * 128:(j + 1) * 128], XT[:, u, j * 128:(j + 1) * 128],
                                                   IDN[:, :])
                    last.then_inc(tout_ps, 1)
                tokens(0)
                tokens(1)
                channels(0)
                tokens(2)
                channels(1)
                tokens(3)
                channels(2)
                channels(3)

            four(0, first=True)
            with pe.Fori(1, 16) as k:
                four(k)
            pe.wait_ge(norm_done, 64)
            pe.wait_ge(w_ld, W_LD)
            pe.wait_ge(consts, 2)
            for h in range(2):
                mm(bank[h][:, :], CEN[:, :], EWRAW[:, 512 * h:512 * h + 512], start=True, stop=True).then_inc(ewc_ps, 1)
            mm(bank[2][:, 0:NE], CEN[:, :], RW[:, :], start=True, stop=True).then_inc(ewc_ps, 1)
            nc.tensor.transpose(bank[3][:, 0:C], FW[:, :], IDN[:, :]).then_inc(ewc_ps, 1)
            pe.wait_ge(ewc_sb, 4)

            pe.wait_ge(sh0_ready, 1)
            for k in range(KI):
                last = mm(bank[7][:, k:k + 1], WIN[:, k * 128:(k + 1) * 128], SH0[:, 0:1], start=True, stop=True)
            last.then_inc(zb_ps, 1)
            pe.wait_ge(zb_ready, 1)
            pe.wait_ge(b_rows, 16 * 3 * KH)
            pe.wait_ge(consts, 14)

            def slot(i, s, on, nxt):
                g, o, n = i - 1, i - LAG["moe"], i - LAG["put"]
                q, l, w = i - LAG["conv"], i - LAG["ln"], i - LAG["wx"]

                def inputs(t, par):
                    pre = bPRE[t % 2]
                    mm(pre[:, 0:128], SEL[:, :], BX[:, :], start=True, stop=False, skip_group_check=True)
                    for k in range(KI):
                        for j in range(KH):
                            mm(pre[B * j:B * j + B, 0:128], INP[:, par, k, t * B:(t + 1) * B],
                               WIH[:, k, j * 128:(j + 1) * 128], start=False, stop=False, skip_group_check=True)

                def step(t):
                    if "rnn" in on:
                        if not (isinstance(i, int) and i == 1 and t == 0):
                            pe.wait_ge(h_sb, STEPS * g + t)
                        ph, pt = (s, STEPS - 1) if t == 0 else (1 - s, t - 1)
                        for k in range(KH):
                            for j in range(KH):
                                last = mm(bPRE[t % 2][B * j:B * j + B, 0:128], H[:, ph, k, pt, :],
                                          WHH[:, k, j * 128:(j + 1) * 128], start=False, stop=(k == KH - 1),
                                          skip_group_check=True)
                        last.then_inc(pre_ready, 1)
                    if t < STEPS - 1 and "rnn" in on:
                        inputs(t + 1, 1 - s)
                    if t == STEPS - 1 and "z" in on:
                        pe.wait_ge(inp_ready, i + 1)
                        inputs(0, s)
                    if "rnn" in on:
                        pe.wait_ge(tanh_done, STEPS * g + t + 1)
                        nc.tensor.transpose(bPRE[t % 2][:, 128:256], HTOK[:, :], IDN[:, :]).then_inc(ht_ps, 1)

                step(0)
                if "put" in on:
                    pe.wait_ge(gt_sb, n + 1)
                    mm(bT[:, 0:C], GT[:, :], EB[:, :], start=False, stop=True, skip_group_check=True).then_inc(acc_ps, 1)
                if "moe" in on:
                    pe.wait_ge(h_sb, STEPS * (o + 1))
                    for k in range(KH):
                        last = mm(bM[:, 0:TOK], WOUT[:, k, :], H[:, s, k, :, :].rearrange("p s b -> p (s b)"),
                                  start=(k == 0), stop=(k == KH - 1))
                    last.then_inc(o_ps, 1)
                if "z" in on:
                    pe.wait_ge(xin_ready, i + 1)
                    if "wx" in on:
                        pe.wait_ge(wxs, w)
                    for k in range(KI):
                        last = mm(bZ[:, k * TOK:(k + 1) * TOK], WINS[:, k * 128:(k + 1) * 128], XIN[:, s, :],
                                  start=True, stop=True)
                    last.then_inc(z_ps, 1)
                step(1)
                if "ln" in on:
                    if "put" in on:
                        pe.wait_ge(acc_sb, n + 1)
                    pe.wait_ge(t3c_ready, l + 1)
                    nc.tensor.transpose(bT[:, 256:256 + C], T3C[:, :], IDN[:, :]).then_inc(t4_ps, 1)
                if "conv" in on:
                    pe.wait_ge(cc_ready, q + 1)
                    if "put" in on:
                        pe.wait_ge(xl_sb, n)
                    else:
                        pe.wait_ge(xl_sb, GROUPS)
                    if "ln" in on:
                        pe.wait_ge(lc_sb, l)

                def taps(a, b):
                    for k in range(a, b):
                        last = mm(bC[:, 0:TOK].rearrange("p (b w) -> p b w", b=IMGS), CW[:, k * C:(k + 1) * C],
                                  CC[:, :, k:k + WW], start=(k == 0), stop=(k == TAPS - 1))
                    return last
                if "conv" in on:
                    taps(0, TAPS - 1)
                step(2)
                if "conv" in on:
                    taps(TAPS - 1, TAPS).then_inc(conv_ps, 1)
                if "moe" in on:
                    pe.wait_ge(tc_ready, o + 1)
                    if "ln" in on:
                        pe.wait_ge(l_tok, l + 1)
                    nc.tensor.transpose(bT[:, 0:C], TC[:, :], IDN[:, :]).then_inc(t1_ps, 1)
                    mm(bM[:, 128:128 + NE], TC[:, :], RWC[:, :], start=True, stop=True).then_inc(rt_ps, 1)
                    if "put" in on:
                        pe.wait_ge(comb_done, n + 1)
                    for h in range(2):
                        last = mm(EPS_BANKS[h][:, :], TC[:, :], EW[:, 512 * h:512 * h + 512], start=True, stop=True)
                    last.then_inc(moe_ps, 1)
                if "wx" in on:
                    if "z" in on:
                        pe.wait_ge(inp_ready, i + 1)
                    else:
                        pe.wait_ge(wxs, w)
                    pe.wait_ge(lc_sb, w + 1)
                    mm(bZ[:, 256:256 + TOK], FWT[:, :], LC[:, :], start=True, stop=True).then_inc(wx_ps, 1)
                step(3)
                if "ln" in on:
                    if "conv" in on:
                        pe.wait_ge(y_ready, q + 1)
                    pe.wait_ge(l_tok, l + 1)
                    nc.tensor.transpose(bC[:, 2 * C:3 * C], LTOK[:, :], IDN[:, :]).then_inc(t5_ps, 1)
                if "put" in on:
                    pe.wait_ge(xlt_ready, n + 1)
                    if "conv" in on:
                        pe.wait_ge(y_ready, q + 1)
                    nc.tensor.transpose(bC[:, 0:C], ACC[:, :], IDN[:, :])
                    nc.tensor.transpose(bC[:, C:2 * C], XLT[:, :], IDN[:, :]).then_inc(t23_ps, 1)
                if "moe" in on:
                    pe.wait_ge(g_ready, o + 1)
                    nc.tensor.transpose(bM[:, 256:256 + TOK], GP[:, :], IDN[:, :]).then_inc(gt_ps, 1)

            run(slot)(pe)

            pe.wait_ge(fws_ready, 1)
            nc.tensor.transpose(bank[7][:, 0:C], FWS[:, :], IDN[:, :]).then_inc(fwst_ps, 1)
            pe.wait_ge(fwst_sb, 1)
            
            def inputs(r, h):
                pe.wait_ge(lr_ld, 16 * (r + 1))
                mm(bank[h][:, MARGIN:MARGIN + 8 * B], FWST[:, :],
                   XR[:, :, :].rearrange("p a n -> p (a n)")[:, bass.ds((r & 1) * L + 8 * B * h, 8 * B)],
                   start=True, stop=True, skip_group_check=True).then_inc(wx2_ps, 1)

            inputs(0, 0)
            inputs(0, 1)

            def row(r, last_row):
                for w in range(WW):
                    new = (w - 1) % WW
                    old = min(new, 3)
                    end = MARGIN + (w % 8 + 1) * B
                    pe.wait_ge(y2, WW * r + w + 1)
                    mm(bank[w // 8][:, end - (old + 1) * B:end], VT[:, :],
                       YS[:, new - old:new + 1, :].rearrange("p w b -> p (w b)"),
                       start=False, stop=True, skip_group_check=True).then_inc(pre2, 1)
                    if w % 8 == 2:
                        if w // 8 < 2:
                            inputs(r, w // 8 + 2)
                        elif not last_row:
                            inputs(r + 1, w // 8 - 2)

            with pe.Fori(0, HH - 1) as r:
                row(r, False)
            row(HH - 1, True)


def kernel(x, L0_conv_gamma, L0_conv_beta, L0_conv_w_in, L0_conv_b_in, L0_conv_w_ih, L0_conv_b_ih, L0_conv_w_hh,
           L0_conv_b_hh, L0_conv_w_out, L0_conv_b_out, L0_ffn_router_w, L0_ffn_router_b, L0_ffn_expert_w,
           L0_ffn_expert_b, L1_conv_kernel, L1_conv_bias, L1_ffn_W, L1_ffn_V, L1_ffn_gamma, L1_ffn_beta):
    import numpy as np
    import concourse.bacc as bacc
    from concourse.bass_utils import run_bass_kernel_spmd

    def parts(w):
        w = np.asarray(w)
        return w.reshape(-1, 128, w.shape[-1]).transpose(1, 0, 2)

    def col(v):
        return np.asarray(v).reshape(-1, 128).T

    def row(v):
        return np.asarray(v).reshape(1, -1)

    ins = dict(
        x=np.asarray(x).reshape(B, C, L),
        w_inT=np.asarray(L0_conv_w_in).T, b_in=col(L0_conv_b_in),
        w_ihT=parts(np.asarray(L0_conv_w_ih).T), b_ih=row(L0_conv_b_ih),
        w_hhT=parts(np.asarray(L0_conv_w_hh).T), b_hh=row(L0_conv_b_hh),
        w_outT=parts(np.asarray(L0_conv_w_out).T), b_out=col(L0_conv_b_out),
        gamma0=col(L0_conv_gamma), beta0=col(L0_conv_beta),
        router_w=np.asarray(L0_ffn_router_w), router_b=np.asarray(L0_ffn_router_b),
        expert_w=np.asarray(L0_ffn_expert_w).transpose(1, 0, 2).reshape(C, NE * C), expert_b=np.asarray(L0_ffn_expert_b),
        conv_w=np.asarray(L1_conv_kernel).reshape(C, TAPS * C), conv_b=col(L1_conv_bias),
        ffn_w=np.asarray(L1_ffn_W), ffn_vT=np.asarray(L1_ffn_V).T,
        gamma1=col(L1_ffn_gamma), beta1=col(L1_ffn_beta))
    nc = bacc.Bacc("TRN2", target_bir_lowering=False, num_devices=1)
    arrays, args = {}, {}
    for name, a in ins.items():
        a = np.ascontiguousarray(a)
        arrays[f"in_{name}"] = a
        args[name] = nc.dram_tensor(f"in_{name}", a.shape, mybir.dt.from_np(a.dtype), kind="ExternalInput").ap()
    lt_rows = nc.dram_tensor("lt_rows", (HH, C, L), F32).ap()
    out = nc.dram_tensor("out", (B, C, L), F32, kind="ExternalOutput").ap()
    metaformer(nc, **args, lt_rows=lt_rows, out=out)
    r = run_bass_kernel_spmd(nc, [arrays], core_ids=[0])
    return r.results[0]["out"].reshape(B, C, HH, WW)
```

```python
import concourse.bass as bass
from concourse import mybir
from contextlib import ExitStack

F32R = mybir.dt.float32r
F32 = mybir.dt.float32
BF16 = mybir.dt.bfloat16
U32 = mybir.dt.uint32
ALU = mybir.AluOpType
ACT = mybir.ActivationFunctionType

B, C, HH, WW = 32, 128, 32, 32
L = HH * WW
STEPS = 4
TOK = STEPS * B
GROUPS = L // STEPS
PER_ROW = WW // STEPS
IMGS = B // PER_ROW
RIN, RH = 256, 512
KI, KH = RIN // 128, RH // 128
NE = 8
TAPS, PAD = 9, 4
EPS_C, EPS_T, EPS_BN = 1e-6, 1e-5, 1e-5

LAG = dict(z=0, rnn=1, moe=2, put=3, conv=PER_ROW + 3, ln=PER_ROW + 5, wx=PER_ROW + 6)


def stages_in(slot):
    return frozenset(s for s, lag in LAG.items() if 0 <= slot - lag < GROUPS)


def segments():
    pairs = (GROUPS + max(LAG.values()) + 1) // 2
    kind = [(stages_in(2 * p), stages_in(2 * p + 1), stages_in(2 * p + 2)) for p in range(pairs)]
    out = []
    for p in range(pairs):
        if out and kind[p] == kind[out[-1][0]]:
            out[-1][1] += 1
        else:
            out.append([p, 1])
    return [tuple(x) for x in out]


def metaformer(nc, x, w_inT, b_in, w_ihT, b_ih, w_hhT, b_hh, w_outT, b_out, gamma0, beta0,
               router_w, router_b, expert_w, expert_b, conv_w, conv_b, ffn_w, ffn_vT, gamma1, beta1,
               lt_rows, out):
    ctx = ExitStack()
    with ctx:
        def sb(name, shape, dt=F32):
            return ctx.enter_context(nc.sbuf_tensor(name, shape, dt))

        def sem(name):
            return ctx.enter_context(nc.semaphore(name))

        X = sb("X", [128, B, L])
        XR = sb("XR", [128, 2, L])
        CI = sb("CI", [128, 2, B, WW])
        Y = sb("Y", [128, B, WW])
        WHH = sb("WHH", [128, KH, RH])
        WIH = sb("WIH", [128, KI, RH])
        WIN = sb("WIN", [128, RIN])
        WINS = sb("WINS", [128, RIN])
        WOUT = sb("WOUT", [128, KH, C])
        EWH, EWL = (sb(n, [128, NE * C], F32R) for n in ("EWH", "EWL"))
        RW = sb("RW", [128, NE])
        CWH, CWL = (sb(n, [128, TAPS * C], F32R) for n in ("CWH", "CWL"))
        FW = sb("FW", [128, C])
        FWT = sb("FWT", [128, C])
        VT = sb("VT", [128, C])
        EB = sb("EB", [NE, C])
        RB = sb("RB", [128, NE])
        BIN = sb("BIN", [128, KI])
        ZB = sb("ZB", [128, KI])
        BOUT = sb("BOUT", [128, 1])
        CB = sb("CB", [128, 1])
        G0, B0, G1, B1 = (sb(n, [128, 1]) for n in ("G0", "B0", "G1", "B1"))
        BX = sb("BX", [3 * KH, 128], BF16)
        SEL = sb("SEL", [3 * KH, KH * B], BF16)
        IDRW = sb("IDRW", [128, 128 + NE])
        IDN, RWC = IDRW[:, 0:128], IDRW[:, 128:128 + NE]
        STX = sb("STX", [128, 2, 4, 6])
        MVX = sb("MVX", [128, 4, 4, 2])
        VX, MX0, RX, NX = (sb(n, [128, 4, 4]) for n in ("VX", "MX0", "RX", "NX"))
        IOTA = sb("IOTA", [128, NE])
        NHALF = sb("NHALF", [128, 4])
        WXS = sb("WXS", [128, GROUPS // 2, 6])
        MV0 = sb("MV0", [128, 2])
        MV4 = sb("MV4", [128, 2])
        R0 = sb("R0", [128, 1])
        R4 = sb("R4", [128, 1])
        SC0, SH0, SC1, SH1, TMP0, TMP1 = (sb(n, [128, 1]) for n in ("SC0", "SH0", "SC1", "SH1", "TMP0", "TMP1"))
        XIN = sb("XIN", [128, 2, TOK])
        TH = sb("TH", [128, KI, TOK])
        INP = sb("INP", [128, 2, KI, TOK])
        HTOK = sb("HTOK", [128, 128])
        H = sb("H", [128, 2, KH, STEPS, B])
        TC = sb("TC", [128, TOK])
        TCH, TCL = (sb(n, [128, TOK], F32R) for n in ("TCH", "TCL"))
        ACC = sb("ACC", [128, C])
        ACC2 = sb("ACC2", [128, C])
        XLT = sb("XLT", [128, C])
        LTOK = sb("LTOK", [128, C])
        T3C = sb("T3C", [128, 2 * TOK])
        LC = sb("LC", [128, TOK])
        CCH, CCL = (sb(n, [128, 2 * IMGS, WW + 2 * PAD], F32R) for n in ("CCH", "CCL"))
        GP = sb("GP", [128, 128])
        GR = sb("GR", [128, NE])
        GA = sb("GA", [128, NE])
        GB = sb("GB", [128, NE])
        GT = sb("GT", [NE, TOK])
        LG = sb("LG", [128, NE])
        MX = sb("MX", [128, 8])
        IX = sb("IX", [128, 8], U32)
        IXF = sb("IXF", [128, 8])
        EX, DN, G_1, G_2 = (sb(n, [128, 1]) for n in ("EX", "DN", "G_1", "G_2"))
        ST1, ST2, ST3 = (sb(n, [128, 6]) for n in ("ST1", "ST2", "ST3"))
        MV1, MV2, MV3 = (sb(n, [128, 2]) for n in ("MV1", "MV2", "MV3"))
        V1, V2, V3, V0, V4 = (sb(n, [128, 1]) for n in ("V1", "V2", "V3", "V0", "V4"))
        R1, R2, R3 = (sb(n, [128, 1]) for n in ("R1", "R2", "R3"))

        bank = [ctx.enter_context(nc.psum_tensor(f"bank{i}", [128, 512], F32)) for i in range(8)]
        bPRE = bank[0:2]
        EPS_BANKS = [bank[2], bank[3]]
        bZ, bC, bT, bM = bank[4], bank[5], bank[6], bank[7]

        WXSF = WXS[:, :, :].rearrange("p t s -> p (t s)")
        BRA = WXSF[0:1, 0:RH]
        BRB = INP[0:1, :, :, :].rearrange("p a k n -> p (a k n)")
        BHI = WXSF[0:1, 512:768].bitcast(BF16)
        BMID = XIN[0:1, :, :].rearrange("p a n -> p (a n)").bitcast(BF16)
        CEN = HTOK
        BLO = TH[0:1, :, :].rearrange("p k n -> p (k n)").bitcast(BF16)
        STAT0 = H[:, 0, :, :, :].rearrange("p k s b -> p (k s b)")[:, 0:64 * 6].rearrange("p (t s) -> p t s", s=6)
        FWS, FWST = T3C[:, 0:C], ACC
        XS = CI[:, :, :, :].rearrange("p a b w -> p (a b w)").rearrange("p (u n) -> p u n", u=4)
        XT = XR[:, :, :].rearrange("p a n -> p (a n)").rearrange("p (u n) -> p u n", u=4)
        EWRAW = Y[:, :, :].rearrange("p b w -> p (b w)")
        XF = X[:, :, :].rearrange("p b l -> p (b l)")
        CWRAW = XF[:, B * L - TAPS * C:B * L]
        YS = Y[:, :, :].rearrange("p b w -> p (b w)").rearrange("p (w b) -> p w b", w=WW)

        x_ld = [sem(f"x_ld{i}") for i in range(4)]
        w_ld = sem("w_ld")
        consts = sem("consts")
        pool_own, dve_own = sem("pool_own"), sem("dve_own")
        (tin_ps, mvx_ready, rx_ready, xt_ready, tout_ps, x_ready, norm_done, ewc_ps, ewc_sb, mv0_ready, r0_ready,
         zb_ps, sh0_ready, zb_ready, ys_zero) = (sem(n) for n in (
             "tin_ps", "mvx_ready", "rx_ready", "xt_ready", "tout_ps", "x_ready", "norm_done", "ewc_ps", "ewc_sb",
             "mv0_ready", "r0_ready",
             "zb_ps", "sh0_ready", "zb_ready", "ys_zero"))
        b_split, b_rows = sem("b_split"), sem("b_rows")
        (xin_ready, z_ps, th_ready, inp_ready, pre_ready, tanh_done, ht_ps, h_sb, o_ps, tc_ready, t1_ps, moe_ps,
         mv1_ready, r1_ready, mx_ready, e_ready, g_ready, gt_ps, gt_sb, acc_ps, acc_sb, comb_done, mv2_ready,
         r2_ready, xlt_ready, t23_ps, xl_sb, cc_ready, conv_ps, y_ready, t3c_ready, t4_ps, mv3_ready, r3_ready,
         l_tok, t5_ps, lc_sb, wx_ps, wxs, spilled, xr_ld) = (sem(n) for n in (
             "xin_ready", "z_ps", "th_ready", "inp_ready", "pre_ready", "tanh_done", "ht_ps", "h_sb", "o_ps", "tc_ready", "t1_ps",
             "moe_ps", "mv1_ready", "r1_ready", "mx_ready", "e_ready", "g_ready", "gt_ps", "gt_sb",
             "acc_ps", "acc_sb", "comb_done", "mv2_ready", "r2_ready", "xlt_ready", "t23_ps", "xl_sb", "cc_ready",
             "conv_ps", "y_ready", "t3c_ready", "t4_ps", "mv3_ready", "r3_ready", "l_tok", "t5_ps", "lc_sb",
             "wx_ps", "wxs", "spilled", "xr_ld"))
        (mv4_ready, r4_ready, fws_ready, fwst_ps, fwst_sb, lr_ld, wx2_ps, pre2, y2, added, stored) = (
            sem(n) for n in ("mv4_ready", "r4_ready", "fws_ready", "fwst_ps", "fwst_sb", "lr_ld", "wx2_ps", "pre2",
                             "y2", "added", "stored"))

        stx, mv_own = sem("stx"), sem("mv_own")
        ci_sum, cch_ready = sem("ci_sum"), sem("cch_ready")
        tch_ready, tcl_ready = sem("tch_ready"), sem("tcl_ready")
        (pv1, pv2, pv3, x3_ready, comb, st1, st2, st3, lg, gate, gr_ready, px1) = (sem(n) for n in (
            "pv1", "pv2", "pv3", "x3_ready", "comb", "st1", "st2", "st3", "lg", "gate", "gr_ready", "px1"))

        SEGS = segments()
        WARM = (512, 512, 384)
        ZERO = INP[:, 0, :, :].rearrange("p k n -> p (k n)").bitcast(BF16)
        weights = [(WHH[:, :, :], w_hhT), (WIH[:, :, :], w_ihT), (WIN[:, :], w_inT), (WOUT[:, :, :], w_outT),
                   (EWRAW, expert_w), (RW[:, :], router_w), (CWRAW, conv_w), (FW[:, :], ffn_w), (VT[:, :], ffn_vT),
                   (EB[:, :], expert_b), (BIN[:, :], b_in), (BOUT[:, :], b_out), (CB[:, :], conv_b),
                   (G0[:, :], gamma0), (B0[:, :], beta0), (G1[:, :], gamma1), (B1[:, :], beta1),
                   (BRA, b_ih), (BRB, b_hh), (RB[:, :], router_b.partition_broadcast(128))]
        W_LD = 16 * len(weights)

        sp_waits, pool_waits, dve_waits = sem("sp_waits"), sem("pool_waits"), sem("dve_waits")

        def wait_first(eng, s, value, count):
            eng.wait_ge(s, value)
            eng.sem_inc(count, 1)

        block = ctx.enter_context(nc.Block())

        def run(body):
            def over(eng):
                for p0, n in SEGS:
                    def pair(p, base):
                        for s in (0, 1):
                            body(p * 2 + s, s, stages_in(base + s), stages_in(base + s + 1))
                    if n == 1:
                        pair(p0, 2 * p0)
                    else:
                        with eng.Fori(p0, p0 + n) as p:
                            pair(p, 2 * p0)
            return over

        CHUNKS = B * L // 512

        def skewed(eng, first, second, lag):
            for t in range(8):
                first(t, t % 4)
                if t >= lag:
                    second(t - lag, (t - lag) % 4)
            with eng.Fori(2, CHUNKS // 4) as k:
                for u in range(4):
                    first(k * 4 + u, u)
                    second(k * 4 + (u - lag), (u - lag) % 4)
            for t in range(CHUNKS - lag, CHUNKS):
                second(t, t % 4)

        @block.sync
        def _(sp):
            def x_chunk(k, u, first=False):
                if not first:
                    wait_first(sp, tin_ps, (k - 1) * 4 + u + 1, sp_waits)
                sp.dma_start(XS[:, u, :], x[bass.ds((k & 15) * 2 + u // 2, 1), :, 512 * (u % 2):512 * (u % 2) + 512
                                            ].rearrange("b c l -> (b c) l")).then_inc(x_ld[u], 16)

            for u in range(4):
                x_chunk(0, u, first=True)
            with sp.Fori(1, 16) as k:
                for u in range(4):
                    x_chunk(k, u)

            sp.wait_ge(b_split, 1)
            for j in range(KH):
                for part, src in enumerate((BHI, BMID, BLO)):
                    sp.dma_start(BX[3 * j + part:3 * j + part + 1, :], src[:, j * 128:(j + 1) * 128]).then_inc(b_rows, 16)

            def some_row(r):
                return r & (HH - 1)

            def xr_load(r):
                wait_first(sp, xr_ld, 16 * r, sp_waits)
                sp.dma_start(xr_row(r), x_row(r)).then_inc(xr_ld, 16)

            def xr_row(r):
                return XR[:, bass.ds(r & 1, 1), :].rearrange("p a (b w) -> p (a b) w", b=B)

            def x_row(r):
                return x[:, :, bass.ds(some_row(r) * WW, WW)].rearrange("b c w -> c b w")

            def row(r, between=None):
                for u in range(PER_ROW):
                    wait_first(sp, lc_sb, PER_ROW * r + u + 1, sp_waits)
                    sp.dma_start(lt_rows[bass.ds(some_row(r), 1), :, u * TOK:(u + 1) * TOK].rearrange("r c n -> (r c) n"),
                                 LC[:, :]).then_inc(spilled, 16)
                    if u == 6 and between:
                        between()

            def lr_load(r):
                wait_first(sp, lr_ld, 16 * r, sp_waits)
                sp.dma_start(XR[:, bass.ds(r & 1, 1), :].rearrange("p a n -> p (a n)"),
                             lt_rows[bass.ds(some_row(r), 1), :, :].rearrange("r c n -> (r c) n")).then_inc(lr_ld, 16)

            def next_x(r):
                wait_first(sp, tc_ready, PER_ROW * (r + 2), sp_waits)
                xr_load(r + 3)

            def first_lt():
                wait_first(sp, tc_ready, GROUPS, sp_waits)
                lr_load(0)
                lr_load(1)

            wait_first(sp, tout_ps, CHUNKS, sp_waits)
            for r in range(3):
                if r == 2:
                    wait_first(sp, tc_ready, PER_ROW, sp_waits)
                xr_load(r)
            with sp.Fori(0, HH - 3) as r:
                row(r, lambda: next_x(r))
            row(HH - 3)
            row(HH - 2, first_lt)
            row(HH - 1)
            wait_first(sp, spilled, 16 * GROUPS, sp_waits)

            def four_rows(q, loads):
                for u in range(loads):
                    wait_first(sp, wx2_ps, 16 * q + 4 * u + 4, sp_waits)
                    lr_load(q * 4 + u + 2)
                wait_first(sp, added, 8 * q + 8, sp_waits)
                sp.dma_start(out[:, :, bass.ds((q & 7) * 4 * WW, 4 * WW)].rearrange("b c l -> c b l"),
                             X[:, :, bass.ds((q & 7) * 4 * WW, 4 * WW)]).then_inc(stored, 16)
            with sp.Fori(0, HH // 4 - 1) as q:
                four_rows(q, 4)
            four_rows(HH // 4 - 1, 2)
            wait_first(sp, stored, 16 * (HH // 4), sp_waits)

        @block.gpsimd
        def _(pool):
            own = [0]

            def link(ins):
                own[0] += 1
                ins.then_inc(pool_own, 1)
                pool.wait_ge(pool_own, own[0])

            link(nc.gpsimd.memset(IDN, 0.0))
            nc.gpsimd.affine_select(out=IDN, in_=IDN, compare_op=ALU.not_equal, fill=1.0, base=0,
                                    pattern=[[-1, 128]], channel_multiplier=1).then_inc(consts, 1)
            pool.wait_ge(consts, 1)
            nc.gpsimd.tensor_scalar(CEN[:, :], IDN, -1.0 / C, None, ALU.add).then_inc(consts, 1)
            for e in range(NE):
                nc.gpsimd.memset(IOTA[:, e:e + 1], float(e)).then_inc(consts, 1)
            link(nc.gpsimd.memset(SEL[:, :], 1.0))
            link(nc.gpsimd.affine_select(out=SEL[:, :], in_=SEL[:, :], compare_op=ALU.is_ge, fill=0.0, base=0,
                                         pattern=[[-3, KH], [0, B]], channel_multiplier=1))
            nc.gpsimd.affine_select(out=SEL[:, :], in_=SEL[:, :], compare_op=ALU.is_ge, fill=0.0, base=2,
                                    pattern=[[3, KH], [0, B]], channel_multiplier=-1).then_inc(consts, 1)
            nc.gpsimd.memset(CCH[:, :, :].bitcast(F32), 0.0)
            nc.gpsimd.memset(CCL[:, :, :].bitcast(F32), 0.0).then_inc(consts, 1)
            nc.gpsimd.memset(GP[:, :], 0.0).then_inc(consts, 1)
            nc.gpsimd.memset(H[:, 1, :, :, :], 0.0).then_inc(consts, 1)
            link(nc.gpsimd.memset(NHALF[:, :], -0.5))

            def rstd(r, v, mv, eps, ready):
                link(nc.gpsimd.tensor_scalar(v[:, :], mv[:, 1:2], eps, None, ALU.add))
                nc.gpsimd.tensor_tensor(r[:, :], v[:, :], NHALF[:, 0:1], ALU.pow).then_inc(ready, 1)

            def deviations(k):
                for u in range(4):
                    t = k * 4 + u
                    pool.wait_ge(mvx_ready, t + 1)
                    nc.gpsimd.tensor_tensor(RX[:, u, :], VX[:, u, :], NHALF[:, :], ALU.pow).then_inc(px1, 1)
                    pool.wait_ge(px1, t + 1)
                    nc.gpsimd.tensor_tensor(NX[:, u, :], MX0[:, u, :], RX[:, u, :], ALU.mult).then_inc(rx_ready, 1)

            with pool.Fori(0, CHUNKS // 8) as k:
                deviations(k)
            pool.wait_ge(w_ld, W_LD)
            link(nc.gpsimd.tensor_copy(CWH[:, :], CWRAW))
            link(nc.gpsimd.tensor_tensor(CWL[:, :], CWRAW, CWH[:, :], ALU.subtract))
            with pool.Fori(CHUNKS // 8, CHUNKS // 4) as k:
                deviations(k)

            pool.wait_ge(ewc_sb, 3)
            nc.gpsimd.memset(Y[:, :, :], 0.0).then_inc(ys_zero, 1)
            pool.wait_ge(mv0_ready, 1)
            rstd(R0, V0, MV0, EPS_BN, r0_ready)

            def gather(i, s):
                nc.gpsimd.tensor_copy(XIN[:, s, :].rearrange("p (s b) -> p s b", s=STEPS),
                                      X[:, :, bass.ds((i & (GROUPS - 1)) * STEPS, STEPS)].rearrange("p b s -> p s b")
                                      ).then_inc(xin_ready, 1)

            pool.wait_ge(norm_done, 64)
            pool.wait_ge(b_rows, 16 * 3 * KH)
            gather(0, 0)

            pool.wait_ge(ys_zero, 1)

            def slot(i, s, on, nxt):
                q, l, n, o = i - LAG["conv"], i - LAG["ln"], i - LAG["put"], i - LAG["moe"]
                first = (s + LAG["conv"]) % 2 == 0
                if "conv" in on:
                    b0, row = ((q >> 1) & (PER_ROW // 2 - 1)) * 2 * IMGS, (q >> 3) & (HH - 1)
                if "conv" in on and first:
                    if "put" in on:
                        pool.wait_ge(xl_sb, n)
                    else:
                        pool.wait_ge(xl_sb, GROUPS)
                    pool.wait_ge(conv_ps, q >> 1)
                    wait_first(pool, y_ready, q >> 1, pool_waits)
                    ci = CI[:, :, :, :].rearrange("p a b w -> p (a b) w")[:, bass.ds((row & 1) * B + b0, 2 * IMGS), :]
                    nc.gpsimd.tensor_tensor(ci, ci, Y[:, bass.ds(b0, 2 * IMGS), :], ALU.add).then_inc(ci_sum, 1)
                    wait_first(pool, ci_sum, (q >> 1) + 1, pool_waits)
                    nc.gpsimd.tensor_copy(CCH[:, :, PAD:PAD + WW], ci).then_inc(cch_ready, 1)
                    wait_first(pool, cch_ready, (q >> 1) + 1, pool_waits)
                    nc.gpsimd.tensor_tensor(CCL[:, :, PAD:PAD + WW], ci, CCH[:, :, PAD:PAD + WW], ALU.subtract
                                            ).then_inc(cc_ready, 1)
                if "z" in nxt:
                    wait_first(pool, z_ps, i, pool_waits)
                    gather(i + 1, 1 - s)
                if "moe" in on:
                    wait_first(pool, tc_ready, o + 1, pool_waits)
                    nc.gpsimd.tensor_copy(TCH[:, :], TC[:, :]).then_inc(tch_ready, 1)
                    pool.wait_ge(tch_ready, o + 1)
                    nc.gpsimd.tensor_tensor(TCL[:, :], TC[:, :], TCH[:, :], ALU.subtract).then_inc(tcl_ready, 1)
                if "ln" in on:
                    wait_first(pool, mv3_ready, l + 1, pool_waits)
                    nc.gpsimd.tensor_scalar(V3[:, :], MV3[:, 1:2], EPS_T, None, ALU.add).then_inc(pv3, 1)
                    pool.wait_ge(pv3, l + 1)
                    nc.gpsimd.tensor_tensor(R3[:, :], V3[:, :], NHALF[:, 0:1], ALU.pow).then_inc(r3_ready, 1)
                if "put" in on:
                    wait_first(pool, mv2_ready, n + 1, pool_waits)
                    nc.gpsimd.tensor_scalar(V2[:, :], MV2[:, 1:2], EPS_C, None, ALU.add).then_inc(pv2, 1)
                    pool.wait_ge(pv2, n + 1)
                    nc.gpsimd.tensor_tensor(R2[:, :], V2[:, :], NHALF[:, 0:1], ALU.pow).then_inc(r2_ready, 1)
                if "moe" in on:
                    wait_first(pool, mv1_ready, o + 1, pool_waits)
                    nc.gpsimd.tensor_scalar(V1[:, :], MV1[:, 1:2], EPS_T, None, ALU.add).then_inc(pv1, 1)
                    pool.wait_ge(pv1, o + 1)
                    nc.gpsimd.tensor_tensor(R1[:, :], V1[:, :], NHALF[:, 0:1], ALU.pow).then_inc(r1_ready, 1)
                if "conv" in on and not first:
                    pool.wait_ge(y_ready, (q >> 1) + 1)
                    wait_first(pool, t4_ps, q - 1, pool_waits)
                    here = X[:, bass.ds(b0, 2 * IMGS), bass.ds(row * WW, WW)]
                    t3 = T3C[:, :].rearrange("p (b w) -> p b w", w=WW)
                    nc.gpsimd.tensor_tensor(t3, here, Y[:, bass.ds(b0, 2 * IMGS), :], ALU.add).then_inc(t3c_ready, 1)
                    wait_first(pool, t3c_ready, (q >> 1) + 1, pool_waits)
                    nc.gpsimd.tensor_copy(here, t3).then_inc(x3_ready, 1)

            run(slot)(pool)
            pool.wait_ge(x3_ready, GROUPS // 2)
            nc.gpsimd.memset(INP[:, 0, :, :], 0.0)
            nc.gpsimd.memset(YS[:, WW - 1, :], 0.0).then_inc(y2, 1)
            pool.wait_ge(mv4_ready, 1)
            rstd(R4, V4, MV4, EPS_BN, r4_ready)

        @block.scalar
        def _(act):
            for dst, src in weights:
                act.dma_start(dst, src).then_inc(w_ld, 16)

            def normed(t, u):
                act.wait_ge(rx_ready, t + 1)
                if not isinstance(t, int) or t >= 4:
                    act.wait_ge(tout_ps, t - 3)
                for j in range(4):
                    last = nc.scalar.activation(XT[:, u, j * 128:(j + 1) * 128], bank[u][:, j * 128:(j + 1) * 128],
                                                ACT.Identity, scale=RX[:, u, j:j + 1], bias=NX[:, u, j:j + 1])
                last.then_inc(xt_ready, 1)

            def evict(t, u):
                act.wait_ge(tout_ps, t + 1)
                nc.scalar.copy(XF[:, bass.ds((t & (CHUNKS - 1)) * 512, 512)], bank[4 + u][:, :]).then_inc(x_ready, 1)

            skewed(act, normed, evict, 3)

            def slot(i, s, on, nxt):
                g, o, n, q, l = i - 1, i - LAG["moe"], i - LAG["put"], i - LAG["conv"], i - LAG["ln"]

                def step(t):
                    if "rnn" in on:
                        act.wait_ge(pre_ready, STEPS * g + t + 1)
                        nc.scalar.activation(HTOK[:, :], bPRE[t % 2][:, 0:128], ACT.Tanh).then_inc(tanh_done, 1)
                        act.wait_ge(ht_ps, STEPS * g + t + 1)
                        nc.scalar.copy(H[:, 1 - s, :, t, :], bPRE[t % 2][:, 128:256].rearrange("p (k b) -> p k b", k=KH)
                                       ).then_inc(h_sb, 1)
                step(0)
                if "put" in on:
                    act.wait_ge(acc_ps, n + 1)
                    act.wait_ge(t23_ps, n)
                    nc.scalar.copy(ACC[:, :], bT[:, 0:C]).then_inc(acc_sb, 1)
                if "z" in on:
                    act.wait_ge(z_ps, i + 1)
                    act.wait_ge(inp_ready, i)
                    for k in range(KI):
                        last = nc.scalar.activation(TH[:, k, :], bZ[:, k * TOK:(k + 1) * TOK], ACT.Tanh,
                                                    bias=ZB[:, k:k + 1])
                    last.then_inc(th_ready, 1)
                step(1)
                step(2)
                if "conv" in on and (s + LAG["conv"]) % 2 == 1:
                    act.wait_ge(conv_ps, (q >> 1) + 1)
                    nc.scalar.activation(Y[:, bass.ds(((q >> 1) & (PER_ROW // 2 - 1)) * 2 * IMGS, 2 * IMGS), :],
                                         bC[:, 0:2 * TOK].rearrange("p (b w) -> p b w", w=WW), ACT.Relu,
                                         bias=CB[:, 0:1]).then_inc(y_ready, 1)
                if "moe" in on:
                    act.wait_ge(mx_ready, o + 1)
                    nc.scalar.activation(EX[:, :], MX[:, 0:1], ACT.Exp, scale=-1.0, bias=MX[:, 1:2]).then_inc(e_ready, 1)
                step(3)
                if "put" in on:
                    act.wait_ge(t23_ps, n + 1)
                    nc.scalar.copy(X[:, :, bass.ds((n & (GROUPS - 1)) * STEPS, STEPS)].rearrange("p b s -> p s b"),
                                   bM[:, 256:256 + TOK].rearrange("p (s b) -> p s b", s=STEPS))
                    nc.scalar.copy(
                        CI[:, :, :, :].rearrange("p a b w -> p (a b) w")[
                            :, bass.ds(((n >> 3) & 1) * B, B), bass.ds((n & (PER_ROW - 1)) * STEPS, STEPS)
                        ].rearrange("p b s -> p s b"),
                        bM[:, 384:384 + TOK].rearrange("p (s b) -> p s b", s=STEPS)).then_inc(xl_sb, 1)
                if "ln" in on:
                    act.wait_ge(t5_ps, l + 1)
                    if "wx" in on:
                        act.wait_ge(wx_ps, l)
                        act.wait_ge(spilled, 16 * l)
                    nc.scalar.copy(LC[:, :], bM[:, 0:TOK]).then_inc(lc_sb, 1)

            run(slot)(act)

            act.wait_ge(fwst_sb, 1)

            def row(r, first=False):
                for w in range(WW):
                    if w % 16 == 15 and not (first and w == 15):
                        act.wait_ge(added, 2 * r + w // 16)
                    act.wait_ge(pre2, WW * r + w + 1)
                    nc.scalar.activation(YS[:, w, :], bank[w // 16][:, (w % 16) * B:(w % 16 + 1) * B], ACT.Sigmoid,
                                         bias=SH1[:, 0:1]).then_inc(y2, 1)

            row(0, first=True)
            with act.Fori(1, HH) as r:
                row(r)

        @block.vector
        def _(dve):
            own = [0]

            def link(ins):
                own[0] += 1
                ins.then_inc(dve_own, 1)
                dve.wait_ge(dve_own, own[0])

            def over_channels(t, u):
                dve.wait_ge(tin_ps, t + 1)
                for j in range(4):
                    last = nc.vector.bn_stats(STX[:, u % 2, j, :], bank[u][:, j * 128:(j + 1) * 128])
                last.then_inc(stx, 1)
                if not isinstance(t, int) or t >= 6:
                    over_tokens(t - 6)
                wait_first(dve, stx, t + 1, dve_waits)
                for j in range(4):
                    last = nc.vector.bn_aggr(MVX[:, u, j, :], STX[:, u % 2, j, :])
                last.then_inc(mv_own, 1)
                dve.wait_ge(mv_own, t + 1)
                nc.vector.tensor_scalar(MX0[:, u, :], MVX[:, u, :, 0], -1.0, None, ALU.mult)
                nc.vector.tensor_scalar(VX[:, u, :], MVX[:, u, :, 1], EPS_C, None, ALU.add).then_inc(mvx_ready, 1)

            def over_tokens(t):
                at = t & (CHUNKS - 1)
                dve.wait_ge(x_ready, t + 1)
                nc.vector.bn_stats(STAT0[:, bass.ds(at, 1), :].rearrange("p t s -> p (t s)"),
                                   XF[:, bass.ds(at * 512, 512)]).then_inc(norm_done, 1)

            for t in range(8):
                over_channels(t, t % 4)
            with dve.Fori(2, CHUNKS // 8) as k:
                for u in range(4):
                    over_channels(k * 4 + u, u)
            dve.wait_ge(w_ld, W_LD)
            link(nc.vector.tensor_tensor(BRA, BRA, BRB, ALU.add))
            link(nc.vector.tensor_copy(BHI[:, :], BRA))
            link(nc.vector.tensor_tensor(BRB, BRA, BHI[:, :], ALU.subtract))
            link(nc.vector.tensor_copy(BMID[:, :], BRB))
            link(nc.vector.tensor_tensor(BRA, BRB, BMID[:, :], ALU.subtract))
            nc.vector.tensor_copy(BLO[:, :], BRA).then_inc(b_split, 1)
            with dve.Fori(CHUNKS // 8, CHUNKS // 4) as k:
                for u in range(4):
                    over_channels(k * 4 + u, u)
            for t in range(CHUNKS - 6, CHUNKS):
                over_tokens(t)
            dve.wait_ge(ewc_ps, 1)
            link(nc.vector.tensor_copy(EWH[:, 0:512], bank[0][:, :]))
            nc.vector.tensor_tensor(EWL[:, 0:512], bank[0][:, :], EWH[:, 0:512], ALU.subtract).then_inc(ewc_sb, 1)
            dve.wait_ge(ewc_ps, 2)
            link(nc.vector.tensor_copy(EWH[:, 512:1024], bank[1][:, :]))
            nc.vector.tensor_tensor(EWL[:, 512:1024], bank[1][:, :], EWH[:, 512:1024], ALU.subtract).then_inc(ewc_sb, 1)
            dve.wait_ge(ewc_ps, 3)
            nc.vector.tensor_copy(RWC, bank[2][:, 0:NE]).then_inc(ewc_sb, 1)
            dve.wait_ge(ewc_ps, 4)
            nc.vector.tensor_copy(FWT[:, :], bank[3][:, 0:C]).then_inc(ewc_sb, 1)

            dve.wait_ge(norm_done, 64)
            nc.vector.bn_aggr(MV0[:, :], STAT0[:, :, :].rearrange("p t s -> p (t s)")).then_inc(mv0_ready, 1)
            dve.wait_ge(r0_ready, 1)
            link(nc.vector.tensor_tensor(SC0[:, :], G0[:, :], R0[:, :], ALU.mult))
            nc.vector.tensor_scalar(WINS[:, :], WIN[:, :], SC0[:, 0:1], None, ALU.mult)
            link(nc.vector.tensor_tensor(TMP0[:, :], MV0[:, 0:1], SC0[:, :], ALU.mult))
            nc.vector.tensor_tensor(SH0[:, :], B0[:, :], TMP0[:, :], ALU.subtract).then_inc(sh0_ready, 1)
            dve.wait_ge(zb_ps, 1)
            nc.vector.tensor_tensor(ZB[:, :], bank[7][:, 0:KI], BIN[:, :], ALU.add).then_inc(zb_ready, 1)
            dve.wait_ge(consts, 14)

            def slot(i, s, on, nxt):
                o, n, l, w = i - LAG["moe"], i - LAG["put"], i - LAG["ln"], i - LAG["wx"]
                if "put" in on:
                    dve.wait_ge(gt_ps, n + 1)
                    nc.vector.tensor_copy(GT[:, :], bM[0:NE, 128:128 + TOK]).then_inc(gt_sb, 1)
                if "moe" in on:
                    dve.wait_ge(o_ps, o + 1)
                    dve.wait_ge(xr_ld, 16 * ((o >> 3) + 1))
                    dve.wait_ge(moe_ps, o)
                    src = XR[:, :, :].rearrange("p a (b w) -> p (a b) w", b=B)[
                        :, bass.ds(((o >> 3) & 1) * B, B), bass.ds((o & (PER_ROW - 1)) * STEPS, STEPS)]
                    nc.vector.scalar_tensor_tensor(
                        TC[:, :].rearrange("p (s b) -> p s b", s=STEPS), bM[:, 0:TOK].rearrange("p (s b) -> p s b", s=STEPS),
                        BOUT[:, 0:1], src.rearrange("p b s -> p s b"), ALU.add, ALU.add).then_inc(tc_ready, 1)
                if "z" in on:
                    dve.wait_ge(th_ready, i + 1)
                    for k in range(KI):
                        last = nc.vector.scalar_tensor_tensor(
                            INP[:, s, k, :], bZ[:, k * TOK:(k + 1) * TOK], ZB[:, k:k + 1], TH[:, k, :],
                            ALU.add, ALU.subtract)
                    last.then_inc(inp_ready, 1)
                def experts(es):
                    for e in es:
                        src = EPS_BANKS[e // 4][:, (e % 4) * C:(e % 4 + 1) * C]
                        acc = (ACC, ACC2)[e % 2]
                        if e >= 2:
                            dve.wait_ge(comb, NE * n + e - 1)
                        if e == 1:
                            ins = nc.vector.tensor_scalar(ACC2[:, :], src, GR[:, 1:2], None, ALU.mult)
                        else:
                            ins = nc.vector.scalar_tensor_tensor(acc[:, :], src, GR[:, e:e + 1], acc[:, :], ALU.mult, ALU.add)
                        ins.then_inc(comb, 1)

                if "put" in on:
                    dve.wait_ge(acc_sb, n + 1)
                    dve.wait_ge(moe_ps, n + 1)
                    experts(range(0, 3))
                if "ln" in on:
                    dve.wait_ge(t4_ps, l + 1)
                    nc.vector.bn_stats(ST3[:, :], bT[:, 256:256 + C]).then_inc(st3, 1)
                if "put" in on:
                    experts(range(3, 4))
                if "ln" in on:
                    wait_first(dve, st3, l + 1, dve_waits)
                    nc.vector.bn_aggr(MV3[:, :], ST3[:, :]).then_inc(mv3_ready, 1)
                if "put" in on:
                    experts(range(4, NE))
                    dve.wait_ge(comb, NE * n + NE)
                    nc.vector.tensor_tensor(ACC[:, :], ACC[:, :], ACC2[:, :], ALU.add).then_inc(comb_done, 1)
                if "ln" in on:
                    dve.wait_ge(r3_ready, l + 1)
                    nc.vector.tensor_scalar(LTOK[:, :], bT[:, 256:256 + C], MV3[:, 0:1], R3[:, 0:1],
                                            ALU.subtract, ALU.mult).then_inc(l_tok, 1)
                if "put" in on:
                    dve.wait_ge(comb_done, n + 1)
                    nc.vector.bn_stats(ST2[:, :], ACC[:, :]).then_inc(st2, 1)
                    wait_first(dve, st2, n + 1, dve_waits)
                    nc.vector.bn_aggr(MV2[:, :], ST2[:, :]).then_inc(mv2_ready, 1)
                if "moe" in on:
                    dve.wait_ge(t1_ps, o + 1)
                    nc.vector.bn_stats(ST1[:, :], bT[:, 0:C]).then_inc(st1, 1)
                    wait_first(dve, st1, o + 1, dve_waits)
                    nc.vector.bn_aggr(MV1[:, :], ST1[:, :]).then_inc(mv1_ready, 1)
                if "put" in on:
                    dve.wait_ge(r2_ready, n + 1)
                    nc.vector.tensor_scalar(XLT[:, :], ACC[:, :], MV2[:, 0:1], R2[:, 0:1], ALU.subtract, ALU.mult
                                            ).then_inc(xlt_ready, 1)
                if "moe" in on:
                    dve.wait_ge(r1_ready, o + 1)
                    nc.vector.scalar_tensor_tensor(LG[:, :], bT[:, C:C + NE], R1[:, 0:1], RB[:, :],
                                                   ALU.mult, ALU.add).then_inc(lg, 1)
                    wait_first(dve, lg, o + 1, dve_waits)
                    nc.vector.max(MX[:, :], LG[:, :]).then_inc(mx_ready, 1)
                    wait_first(dve, mx_ready, o + 1, dve_waits)
                    nc.vector.max_index(IX[:, :], MX[:, :], LG[:, :]).then_inc(gate, 1)
                    dve.wait_ge(gate, 5 * o + 1)
                    dve.wait_ge(e_ready, o + 1)
                    nc.vector.tensor_copy(IXF[:, :], IX[:, :])
                    nc.vector.tensor_scalar(DN[:, :], EX[:, :], 1.0, None, ALU.add).then_inc(gate, 1)
                    dve.wait_ge(gate, 5 * o + 2)
                    nc.vector.reciprocal(G_1[:, :], DN[:, :]).then_inc(gate, 1)
                    dve.wait_ge(gate, 5 * o + 3)
                    nc.vector.tensor_tensor(G_2[:, :], EX[:, :], G_1[:, :], ALU.mult)
                    nc.vector.tensor_scalar(GA[:, :], IOTA[:, :], IXF[:, 0:1], G_1[:, 0:1], ALU.is_equal, ALU.mult
                                            ).then_inc(gate, 1)
                    dve.wait_ge(gate, 5 * o + 4)
                    nc.vector.tensor_scalar(GB[:, :], IOTA[:, :], IXF[:, 1:2], G_2[:, 0:1], ALU.is_equal, ALU.mult
                                            ).then_inc(gate, 1)
                    dve.wait_ge(gate, 5 * o + 5)
                    nc.vector.tensor_tensor(GP[:, 0:NE], GA[:, :], GB[:, :], ALU.add).then_inc(g_ready, 1)
                    dve.wait_ge(g_ready, o + 1)
                    nc.vector.tensor_scalar(GR[:, :], GP[:, 0:NE], R1[:, 0:1], None, ALU.mult).then_inc(gr_ready, 1)
                    dve.wait_ge(gr_ready, o + 1)
                if "wx" in on and s != LAG["wx"] % 2:
                    dve.wait_ge(wx_ps, w + 1)
                    nc.vector.bn_stats(WXS[:, bass.ds((w >> 1) & (GROUPS // 2 - 1), 1), :].rearrange("p t s -> p (t s)"),
                                       bZ[:, 256:256 + 2 * TOK]).then_inc(wxs, 1)

            run(slot)(dve)
            dve.wait_ge(wxs, GROUPS // 2)
            nc.vector.bn_aggr(MV4[:, :], WXS[:, :, :].rearrange("p t s -> p (t s)")).then_inc(mv4_ready, 1)
            dve.wait_ge(r4_ready, 1)
            link(nc.vector.tensor_tensor(SC1[:, :], G1[:, :], R4[:, :], ALU.mult))
            nc.vector.tensor_scalar(FWS, FW[:, :], SC1[:, 0:1], None, ALU.mult).then_inc(fws_ready, 1)
            link(nc.vector.tensor_tensor(TMP1[:, :], MV4[:, 0:1], SC1[:, :], ALU.mult))
            link(nc.vector.tensor_tensor(SH1[:, :], B1[:, :], TMP1[:, :], ALU.subtract))
            dve.wait_ge(fwst_ps, 1)
            nc.vector.tensor_copy(FWST[:, :], bank[7][:, 0:C]).then_inc(fwst_sb, 1)

            with dve.Fori(0, HH) as r:
                for h in range(2):
                    dve.wait_ge(y2, WW * r + 16 * (h + 1) + 1)
                    here = X[:, :, bass.ds((r & (HH - 1)) * WW + 16 * h, 16)]
                    nc.vector.tensor_tensor(here, here, YS[:, 16 * h:16 * h + 16, :].rearrange("p w b -> p b w"),
                                            ALU.add).then_inc(added, 1)

        @block.tensor
        def _(pe):
            mm = nc.tensor.matmul
            pe.wait_ge(consts, 1)

            def tokens(t, u):
                pe.wait_ge(x_ld[u], 16 * (t // 4 + 1) if isinstance(t, int) else 4 * (t - u) + 16)
                if not isinstance(t, int) or t >= 4:
                    pe.wait_ge(xt_ready, t - 3)
                for j in range(4):
                    last = nc.tensor.transpose(bank[u][:, j * 128:(j + 1) * 128], XS[:, u, j * 128:(j + 1) * 128],
                                               IDN)
                last.then_inc(tin_ps, 1)

            def channels(t, u):
                pe.wait_ge(xt_ready, t + 1)
                if not isinstance(t, int) or t >= 4:
                    pe.wait_ge(x_ready, t - 3)
                for j in range(4):
                    last = nc.tensor.transpose(bank[4 + u][:, j * 128:(j + 1) * 128], XT[:, u, j * 128:(j + 1) * 128],
                                               IDN)
                last.then_inc(tout_ps, 1)

            skewed(pe, tokens, channels, 4)
            pe.wait_ge(norm_done, 64)
            pe.wait_ge(w_ld, W_LD)
            pe.wait_ge(consts, 2)
            for h in range(2):
                mm(bank[h][:, :], CEN[:, :], EWRAW[:, 512 * h:512 * h + 512], start=True, stop=True).then_inc(ewc_ps, 1)
            mm(bank[2][:, 0:NE], CEN[:, :], RW[:, :], start=True, stop=True).then_inc(ewc_ps, 1)
            nc.tensor.transpose(bank[3][:, 0:C], FW[:, :], IDN).then_inc(ewc_ps, 1)
            pe.wait_ge(ewc_sb, 4)

            pe.wait_ge(sh0_ready, 1)
            for k in range(KI):
                last = mm(bank[7][:, k:k + 1], WIN[:, k * 128:(k + 1) * 128], SH0[:, 0:1], start=True, stop=True)
            last.then_inc(zb_ps, 1)
            pe.wait_ge(zb_ready, 1)
            pe.wait_ge(b_rows, 16 * 3 * KH)
            pe.wait_ge(consts, 14)

            def slot(i, s, on, nxt):
                g, o, n = i - 1, i - LAG["moe"], i - LAG["put"]
                q, l, w = i - LAG["conv"], i - LAG["ln"], i - LAG["wx"]

                def gates():
                    if "put" in on:
                        pe.wait_ge(g_ready, n + 1)
                        if not (isinstance(n, int) and n == 0):
                            pe.wait_ge(xl_sb, n)
                        if "ln" in on:
                            pe.wait_ge(lc_sb, l)
                        nc.tensor.transpose(bM[:, 128:128 + TOK], GP[:, :], IDN).then_inc(gt_ps, 1)

                def inputs(t, par, between=None):
                    pre = bPRE[t % 2]
                    mm(pre[:, 0:128], SEL[:, :], BX[:, :], start=True, stop=False, skip_group_check=True)
                    for k in range(KI):
                        for j in range(KH):
                            mm(pre[B * j:B * j + B, 0:128], INP[:, par, k, t * B:(t + 1) * B],
                               WIH[:, k, j * 128:(j + 1) * 128], start=False, stop=False, skip_group_check=True)
                        if k == 0 and between:
                            between()

                def step(t):
                    if "rnn" in on:
                        if not (isinstance(i, int) and i == 1 and t == 0):
                            pe.wait_ge(h_sb, STEPS * g + t)
                        ph, pt = (s, STEPS - 1) if t == 0 else (1 - s, t - 1)
                        for k in range(KH):
                            for j in range(KH):
                                last = mm(bPRE[t % 2][B * j:B * j + B, 0:128], H[:, ph, k, pt, :],
                                          WHH[:, k, j * 128:(j + 1) * 128], start=False, stop=(k == KH - 1),
                                          skip_group_check=True)
                        last.then_inc(pre_ready, 1)
                    if t < STEPS - 1 and "rnn" in on:
                        inputs(t + 1, 1 - s, gates if t == 0 else None)
                    elif t == 0:
                        gates()
                    if t == STEPS - 1 and "z" in on:
                        pe.wait_ge(inp_ready, i + 1)
                        inputs(0, s)
                    if "rnn" in on:
                        pe.wait_ge(tanh_done, STEPS * g + t + 1)
                        nc.tensor.transpose(bPRE[t % 2][:, 128:256], HTOK[:, :], IDN).then_inc(ht_ps, 1)

                step(0)
                if "z" in on:
                    pe.wait_ge(xin_ready, i + 1)
                    if "wx" in on:
                        pe.wait_ge(wxs, w >> 1)
                    for k in range(KI):
                        last = mm(bZ[:, k * TOK:(k + 1) * TOK], WINS[:, k * 128:(k + 1) * 128], XIN[:, s, :],
                                  start=True, stop=True)
                    last.then_inc(z_ps, 1)
                if "put" in on:
                    pe.wait_ge(gt_sb, n + 1)
                    mm(bT[:, 0:C], GT[:, :], EB[:, :], start=False, stop=True, skip_group_check=True).then_inc(acc_ps, 1)
                if "moe" in on:
                    pe.wait_ge(h_sb, STEPS * (o + 1))
                    for k in range(KH):
                        last = mm(bM[:, 0:TOK], WOUT[:, k, :], H[:, s, k, :, :].rearrange("p s b -> p (s b)"),
                                  start=(k == 0), stop=(k == KH - 1))
                    last.then_inc(o_ps, 1)
                step(1)
                if "ln" in on:
                    if "put" in on:
                        pe.wait_ge(acc_sb, n + 1)
                    pe.wait_ge(t3c_ready, (l >> 1) + 1)
                    half = TOK * ((s + LAG["ln"]) % 2)
                    nc.tensor.transpose(bT[:, 256:256 + C], T3C[:, half:half + TOK], IDN).then_inc(t4_ps, 1)
                second, split = (s + LAG["conv"]) % 2, 3 * 5
                if "conv" in on and not second:
                    pe.wait_ge(cch_ready, (q >> 1) + 1)
                    pe.wait_ge(y_ready, q >> 1)

                def expert_part(p):
                    h, k = p // 3, p % 3
                    tok, w4 = ((TCH, EWH), (TCH, EWL), (TCL, EWH))[k]
                    return mm(EPS_BANKS[h][:, :], tok[:, :], w4[:, 512 * h:512 * h + 512], start=(k == 0), stop=(k == 2))

                def taps(a, b):
                    for k in range(a, b):
                        w4, tok = ((CWH, CCH), (CWH, CCL), (CWL, CCH))[k % 3]
                        at = k // 3
                        last = mm(bC[:, 0:2 * TOK].rearrange("p (b w) -> p b w", w=WW), w4[:, at * C:(at + 1) * C],
                                  tok[:, :, at:at + WW], start=(k == 0), stop=(k == 3 * TAPS - 1))
                    return last
                if "conv" in on and second:
                    taps(split, 3 * TAPS - 2)
                elif "conv" in on:
                    taps(0, 1)
                    pe.wait_ge(cc_ready, (q >> 1) + 1)
                    taps(1, split - 2)
                step(2)
                if "conv" in on:
                    if second:
                        taps(3 * TAPS - 2, 3 * TAPS).then_inc(conv_ps, 1)
                    else:
                        taps(split - 2, split)
                if "moe" in on:
                    pe.wait_ge(tc_ready, o + 1)
                    if "ln" in on:
                        pe.wait_ge(l_tok, l + 1)
                    mm(bT[:, 0:C + NE], TC[:, :], IDRW[:, :], start=True, stop=True, skip_group_check=True
                       ).then_inc(t1_ps, 1)
                    if "put" in on:
                        pe.wait_ge(comb_done, n + 1)
                    pe.wait_ge(tcl_ready, o + 1)
                    for p in range(5):
                        expert_part(p)
                step(3)
                if "wx" in on:
                    if "z" in on:
                        pe.wait_ge(inp_ready, i + 1)
                    else:
                        pe.wait_ge(wxs, w >> 1)
                    pe.wait_ge(lc_sb, w + 1)
                    half = TOK * ((s + LAG["wx"]) % 2)
                    mm(bZ[:, 256 + half:256 + half + TOK], FWT[:, :], LC[:, :], start=True, stop=True).then_inc(wx_ps, 1)
                if "moe" in on:
                    expert_part(5).then_inc(moe_ps, 1)
                if "ln" in on:
                    if "put" not in on:
                        pe.wait_ge(lc_sb, l)
                    pe.wait_ge(l_tok, l + 1)
                    nc.tensor.transpose(bM[:, 0:TOK], LTOK[:, :], IDN).then_inc(t5_ps, 1)
                if "put" in on:
                    pe.wait_ge(xlt_ready, n + 1)
                    nc.tensor.transpose(bM[:, 256:256 + TOK], ACC[:, :], IDN)
                    nc.tensor.transpose(bM[:, 384:384 + TOK], XLT[:, :], IDN).then_inc(t23_ps, 1)

            run(slot)(pe)

            pe.wait_ge(fws_ready, 1)
            nc.tensor.transpose(bank[7][:, 0:C], FWS, IDN).then_inc(fwst_ps, 1)
            pe.wait_ge(fwst_sb, 1)

            def inputs(r, quarter):
                pe.wait_ge(lr_ld, 16 * (r + 1))
                at = 8 * B * (quarter % 2)
                src = XR[:, bass.ds(r & 1, 1), :].rearrange("p a (b w) -> p (a b) w", b=B)[
                    :, :, 8 * quarter:8 * quarter + 8].rearrange("p b w -> p w b")
                mm(bank[quarter // 2][:, at:at + 8 * B].rearrange("p (w b) -> p w b", b=B), FWST[:, :],
                   src, start=(quarter % 2 == 0), stop=True, skip_group_check=True).then_inc(wx2_ps, 1)

            inputs(0, 0)
            inputs(0, 1)

            def zeros(cols):
                mm(bank[6][:, 0:cols], ZERO[:, 0:128], ZERO[:, 0:cols], start=True, stop=True)

            def row(r, last_row):
                for w in range(WW):
                    pe.wait_ge(y2, WW * r + w + 1)
                    mm(bank[w // 16][:, (w % 16) * B:(w % 16 + 1) * B], VT[:, :], YS[:, (w - 1) % WW, :],
                       start=False, stop=True, skip_group_check=True).then_inc(pre2, 1)
                    if w in (4, 8):
                        inputs(r, 2 + w // 8)
                    elif w in (20, 24) and not last_row:
                        inputs(r + 1, w // 8 - 2)
                    else:
                        for cols in WARM:
                            zeros(cols)

            with pe.Fori(0, HH - 1) as r:
                row(r, False)
            row(HH - 1, True)


def kernel(x, L0_conv_gamma, L0_conv_beta, L0_conv_w_in, L0_conv_b_in, L0_conv_w_ih, L0_conv_b_ih, L0_conv_w_hh,
           L0_conv_b_hh, L0_conv_w_out, L0_conv_b_out, L0_ffn_router_w, L0_ffn_router_b, L0_ffn_expert_w,
           L0_ffn_expert_b, L1_conv_kernel, L1_conv_bias, L1_ffn_W, L1_ffn_V, L1_ffn_gamma, L1_ffn_beta):
    import numpy as np
    import concourse.bacc as bacc
    from concourse.bass_utils import run_bass_kernel_spmd

    def parts(w):
        w = np.asarray(w)
        return w.reshape(-1, 128, w.shape[-1]).transpose(1, 0, 2)

    def col(v):
        return np.asarray(v).reshape(-1, 128).T

    def row(v):
        return np.asarray(v).reshape(1, -1)

    ins = dict(
        x=np.asarray(x).reshape(B, C, L),
        w_inT=np.asarray(L0_conv_w_in).T, b_in=col(L0_conv_b_in),
        w_ihT=parts(np.asarray(L0_conv_w_ih).T), b_ih=row(L0_conv_b_ih),
        w_hhT=parts(np.asarray(L0_conv_w_hh).T), b_hh=row(L0_conv_b_hh),
        w_outT=parts(np.asarray(L0_conv_w_out).T), b_out=col(L0_conv_b_out),
        gamma0=col(L0_conv_gamma), beta0=col(L0_conv_beta),
        router_w=np.asarray(L0_ffn_router_w), router_b=np.asarray(L0_ffn_router_b),
        expert_w=np.asarray(L0_ffn_expert_w).transpose(1, 0, 2).reshape(C, NE * C), expert_b=np.asarray(L0_ffn_expert_b),
        conv_w=np.asarray(L1_conv_kernel).reshape(C, TAPS * C), conv_b=col(L1_conv_bias),
        ffn_w=np.asarray(L1_ffn_W), ffn_vT=np.asarray(L1_ffn_V).T,
        gamma1=col(L1_ffn_gamma), beta1=col(L1_ffn_beta))
    nc = bacc.Bacc("TRN2", target_bir_lowering=False, num_devices=1)
    arrays, args = {}, {}
    for name, a in ins.items():
        a = np.ascontiguousarray(a)
        arrays[f"in_{name}"] = a
        args[name] = nc.dram_tensor(f"in_{name}", a.shape, mybir.dt.from_np(a.dtype), kind="ExternalInput").ap()
    lt_rows = nc.dram_tensor("lt_rows", (HH, C, L), F32).ap()
    out = nc.dram_tensor("out", (B, C, L), F32, kind="ExternalOutput").ap()
    metaformer(nc, **args, lt_rows=lt_rows, out=out)
    r = run_bass_kernel_spmd(nc, [arrays], core_ids=[0])
    return r.results[0]["out"].reshape(B, C, HH, WW)
```
